# Optimizing a Trainium2 kernel written in Bass

```python
import numpy as np
import jax
import jax.numpy as jnp

def _softmax(x, axis=-1):
    return jax.nn.softmax(x, axis=axis)

def _gelu(x):
    return jax.nn.gelu(x, approximate=True)

def _silu(x):
    return jax.nn.silu(x)

def _sigmoid(x):
    return jax.nn.sigmoid(x)

def _layernorm(x, axis=-1, eps=1e-05):
    m = jnp.mean(x, axis=axis, keepdims=True)
    v = jnp.var(x, axis=axis, keepdims=True)
    return (x - m) / jnp.sqrt(v + eps)

def _scatter_add(tgt, idx, src, axis=0):
    return tgt.at[idx].add(src)

def _segment_sum(src, seg, n):
    return jax.ops.segment_sum(src, seg, n)
kernel_name = 'mk_lm_tower_d2_tok_ids768_r4_c98f64'

def setup_inputs(seed: int=0):
    np.random.seed(seed)
    _w = jnp.asarray

    def _rec_inputs():
        import jax
        import jax.numpy as jnp
        _rk = jax.random.key(seed)
        x = jax.random.randint(jax.random.fold_in(_rk, 1), (8, 256), 0, 31993, jnp.int32)
        mask_BS_i1_0 = jnp.where(jnp.ones((8, 256), dtype=bool), 1, 0).astype(jnp.int32)
        return (x, mask_BS_i1_0)
    x, mask_BS_i1_0 = _rec_inputs()

    def _L0_tok_setup():
        import jax, jax.numpy as jnp
        import numpy as np
        NH = 12
        W = 64
        EPS = 1e-12

        def layer_norm(x, s, b):
            mu = x.mean(-1, keepdims=True)
            var = ((x - mu) ** 2).mean(-1, keepdims=True)
            return (x - mu) / jnp.sqrt(var + EPS) * s + b

        def band_attention(q, k, v, mask):
            B, H, S, d = q.shape
            nc = S // W
            kp = jnp.pad(k, ((0, 0), (0, 0), (W, W), (0, 0)))
            vp = jnp.pad(v, ((0, 0), (0, 0), (W, W), (0, 0)))
            idx = jnp.arange(nc)[:, None] * W + jnp.arange(3 * W)[None, :]
            kb = kp[:, :, idx]
            vb = vp[:, :, idx]
            qc = q.reshape(B, H, nc, W, d)
            scores = jnp.einsum('bhcqd,bhckd->bhcqk', qc, kb) / jnp.sqrt(jnp.asarray(d, q.dtype))
            rel = jnp.arange(3 * W)[None, :] - W - jnp.arange(W)[:, None]
            band_ok = jnp.abs(rel) <= W
            key_abs = idx - W
            pos_ok = (key_abs >= 0) & (key_abs < S)
            mp = jnp.pad(mask, ((0, 0), (W, W)))
            mb = mp[:, idx] > 0
            allowed = mb[:, None, :, None, :] & pos_ok[None, None, :, None, :] & band_ok[None, None, None, :, :]
            scores = jnp.where(allowed, scores, jnp.asarray(-1000000000.0, scores.dtype))
            probs = jax.nn.softmax(scores, axis=-1)
            out = jnp.einsum('bhcqk,bhckd->bhcqd', probs, vb)
            return out.reshape(B, H, S, d)

        def _forward(input_ids, attention_mask, emb_word, emb_pos, emb_ln_s, emb_ln_b, Wq, bq, Wk, bk, Wv, bv, Wo, bo, ln1_s, ln1_b, W1, b1, W2, b2, ln2_s, ln2_b):
            B, S = input_ids.shape
            Hd = emb_word.shape[1]
            dh = Hd // NH
            mask = attention_mask.astype(emb_word.dtype)
            h = layer_norm(emb_word[input_ids] + emb_pos[:S][None], emb_ln_s, emb_ln_b)
            L = Wq.shape[0]
            for l in range(L):

                def heads(x):
                    return x.reshape(B, S, NH, dh).transpose(0, 2, 1, 3)
                q = heads(h @ Wq[l] + bq[l])
                k = heads(h @ Wk[l] + bk[l])
                v = heads(h @ Wv[l] + bv[l])
                a = band_attention(q, k, v, mask)
                a = a.transpose(0, 2, 1, 3).reshape(B, S, Hd)
                h = layer_norm(h + a @ Wo[l] + bo[l], ln1_s[l], ln1_b[l])
                f = jax.nn.gelu(h @ W1[l] + b1[l], approximate=False)
                h = layer_norm(h + f @ W2[l] + b2[l], ln2_s[l], ln2_b[l])
            return h
        key = jax.random.key(seed)
        B, S, Hd, L, V, FF = (2, 1024, 192, 4, 8000, 4 * 192)
        ks = jax.random.split(key, 16)
        std = 0.02
        inp = {'input_ids': jax.random.randint(ks[0], (B, S), 0, V, dtype=jnp.int64) if jax.config.jax_enable_x64 else jax.random.randint(ks[0], (B, S), 0, V, dtype=jnp.int32), 'attention_mask': jnp.ones((B, S), dtype=jnp.int32), 'emb_word': jax.random.normal(ks[1], (V, Hd), jnp.float32) * std, 'emb_pos': jax.random.normal(ks[2], (S, Hd), jnp.float32) * std, 'emb_ln_s': jnp.ones((Hd,), jnp.float32), 'emb_ln_b': jnp.zeros((Hd,), jnp.float32), 'Wq': jax.random.normal(ks[3], (L, Hd, Hd), jnp.float32) * std, 'bq': jnp.zeros((L, Hd), jnp.float32), 'Wk': jax.random.normal(ks[4], (L, Hd, Hd), jnp.float32) * std, 'bk': jnp.zeros((L, Hd), jnp.float32), 'Wv': jax.random.normal(ks[5], (L, Hd, Hd), jnp.float32) * std, 'bv': jnp.zeros((L, Hd), jnp.float32), 'Wo': jax.random.normal(ks[6], (L, Hd, Hd), jnp.float32) * std, 'bo': jnp.zeros((L, Hd), jnp.float32), 'ln1_s': jnp.ones((L, Hd), jnp.float32), 'ln1_b': jnp.zeros((L, Hd), jnp.float32), 'W1': jax.random.normal(ks[7], (L, Hd, FF), jnp.float32) * std, 'b1': jnp.zeros((L, FF), jnp.float32), 'W2': jax.random.normal(ks[8], (L, FF, Hd), jnp.float32) * std, 'b2': jnp.zeros((L, Hd), jnp.float32), 'ln2_s': jnp.ones((L, Hd), jnp.float32), 'ln2_b': jnp.zeros((L, Hd), jnp.float32)}
        return inp
    _L0_tok_all = _L0_tok_setup()
    _L0_tok_in = {k: v for k, v in _L0_tok_all.items() if k in ('emb_word', 'emb_pos', 'emb_ln_s', 'emb_ln_b', 'Wq', 'bq', 'Wk', 'bk', 'Wv', 'bv', 'Wo', 'bo', 'ln1_s', 'ln1_b', 'W1', 'b1', 'W2', 'b2', 'ln2_s', 'ln2_b')}
    del _L0_tok_all

    def _L0_attn_setup():
        import jax, jax.numpy as jnp
        import numpy as np
        B, N, C, H = (8, 1024, 192, 8)
        key = jax.random.key(seed)
        k1, k2, k3 = jax.random.split(key, 3)
        x = jax.random.normal(k1, (B, N, C), dtype=jnp.float32)
        W_qkv = jax.random.normal(k2, (C, 3 * C), dtype=jnp.float32) * 0.02
        W_proj = jax.random.normal(k3, (C, C), dtype=jnp.float32) * 0.02
        b_proj = jnp.zeros((C,), dtype=jnp.float32)
        temp = jnp.ones((H, 1, 1), dtype=jnp.float32)
        return {'x': x, 'W_qkv': W_qkv, 'W_proj': W_proj, 'b_proj': b_proj, 'temp': temp}
    _L0_attn_all = _L0_attn_setup()
    _L0_attn_in = {k: v for k, v in _L0_attn_all.items() if k in ('W_qkv', 'W_proj', 'b_proj', 'temp')}
    del _L0_attn_all

    def _L0_ffn_setup():
        import jax, jax.numpy as jnp
        import numpy as np
        B, T, E = (2, 256, 192)
        H = 768
        N_EXP = 4
        key = jax.random.key(seed)
        ks = jax.random.split(key, 8)
        s_e = 1.0 / np.sqrt(E)
        s_h = 1.0 / np.sqrt(H)
        return {'x': jax.random.normal(ks[0], (B, T, E), dtype=jnp.float32), 'Wg': jax.random.uniform(ks[1], (E, N_EXP), minval=-s_e, maxval=s_e, dtype=jnp.float32), 'bg': jax.random.uniform(ks[2], (N_EXP,), minval=-s_e, maxval=s_e, dtype=jnp.float32), 'W1': jax.random.uniform(ks[3], (N_EXP, E, H), minval=-s_e, maxval=s_e, dtype=jnp.float32), 'b1': jax.random.uniform(ks[4], (N_EXP, H), minval=-s_e, maxval=s_e, dtype=jnp.float32), 'W2': jax.random.uniform(ks[5], (N_EXP, H, E), minval=-s_h, maxval=s_h, dtype=jnp.float32), 'b2': jax.random.uniform(ks[6], (N_EXP, E), minval=-s_h, maxval=s_h, dtype=jnp.float32)}
    _L0_ffn_all = _L0_ffn_setup()
    _L0_ffn_in = {k: v for k, v in _L0_ffn_all.items() if k in ('Wg', 'bg', 'W1', 'b1', 'W2', 'b2')}
    del _L0_ffn_all

    def _L1_attn_setup():
        import jax, jax.numpy as jnp
        import numpy as np
        HEADS = 12
        DIM = 192
        HEAD_DIM = DIM // HEADS
        SCALE = HEAD_DIM ** (-0.5)
        key = jax.random.key(seed)
        k_x, k_qkv, k_proj, k_b = jax.random.split(key, 4)
        B, S = (4, 512)
        x = jax.random.normal(k_x, (B, S, DIM), dtype=jnp.float32)
        Wqkv = jax.random.normal(k_qkv, (DIM, 3 * DIM), dtype=jnp.float32) * DIM ** (-0.5)
        Wproj = jax.random.normal(k_proj, (DIM, DIM), dtype=jnp.float32) * DIM ** (-0.5)
        bproj = jax.random.normal(k_b, (DIM,), dtype=jnp.float32) * 0.01
        return {'x': x, 'Wqkv': Wqkv, 'Wproj': Wproj, 'bproj': bproj}
    _L1_attn_all = _L1_attn_setup()
    _L1_attn_in = {k: v for k, v in _L1_attn_all.items() if k in ('Wqkv', 'Wproj', 'bproj')}
    del _L1_attn_all

    def _L1_ffn_setup():
        import jax, jax.numpy as jnp
        import numpy as np
        E = 8
        K = 2
        D = 192
        F = 4 * D
        key = jax.random.key(seed)
        ks = jax.random.split(key, 10)
        s_exp = 0.02
        return {'x': jax.random.normal(ks[0], (4, 256, D), jnp.float32), 'W1': jax.random.normal(ks[1], (E, F, D), jnp.float32) * s_exp, 'b1': jax.random.normal(ks[2], (E, F), jnp.float32) * s_exp, 'W2': jax.random.normal(ks[3], (E, D, F), jnp.float32) * s_exp, 'b2': jax.random.normal(ks[4], (E, D), jnp.float32) * s_exp, 'Wr1': jax.random.normal(ks[5], (D, D), jnp.float32) * s_exp, 'br1': jax.random.normal(ks[6], (D,), jnp.float32) * s_exp, 'Wr2': jax.random.normal(ks[7], (E, D), jnp.float32) * s_exp, 'br2': jax.random.normal(ks[8], (E,), jnp.float32) * s_exp}
    _L1_ffn_all = _L1_ffn_setup()
    _L1_ffn_in = {k: v for k, v in _L1_ffn_all.items() if k in ('W1', 'b1', 'W2', 'b2', 'Wr1', 'br1', 'Wr2', 'br2')}
    del _L1_ffn_all
    return {'x': x, 'mask_BS_i1_0': mask_BS_i1_0, 'L0_tok_emb_word': _L0_tok_in['emb_word'], 'L0_tok_emb_pos': _L0_tok_in['emb_pos'], 'L0_tok_emb_ln_s': _L0_tok_in['emb_ln_s'], 'L0_tok_emb_ln_b': _L0_tok_in['emb_ln_b'], 'L0_tok_Wq': _L0_tok_in['Wq'], 'L0_tok_bq': _L0_tok_in['bq'], 'L0_tok_Wk': _L0_tok_in['Wk'], 'L0_tok_bk': _L0_tok_in['bk'], 'L0_tok_Wv': _L0_tok_in['Wv'], 'L0_tok_bv': _L0_tok_in['bv'], 'L0_tok_Wo': _L0_tok_in['Wo'], 'L0_tok_bo': _L0_tok_in['bo'], 'L0_tok_ln1_s': _L0_tok_in['ln1_s'], 'L0_tok_ln1_b': _L0_tok_in['ln1_b'], 'L0_tok_W1': _L0_tok_in['W1'], 'L0_tok_b1': _L0_tok_in['b1'], 'L0_tok_W2': _L0_tok_in['W2'], 'L0_tok_b2': _L0_tok_in['b2'], 'L0_tok_ln2_s': _L0_tok_in['ln2_s'], 'L0_tok_ln2_b': _L0_tok_in['ln2_b'], 'L0_attn_W_qkv': _L0_attn_in['W_qkv'], 'L0_attn_W_proj': _L0_attn_in['W_proj'], 'L0_attn_b_proj': _L0_attn_in['b_proj'], 'L0_attn_temp': _L0_attn_in['temp'], 'L0_ffn_Wg': _L0_ffn_in['Wg'], 'L0_ffn_bg': _L0_ffn_in['bg'], 'L0_ffn_W1': _L0_ffn_in['W1'], 'L0_ffn_b1': _L0_ffn_in['b1'], 'L0_ffn_W2': _L0_ffn_in['W2'], 'L0_ffn_b2': _L0_ffn_in['b2'], 'L1_attn_Wqkv': _L1_attn_in['Wqkv'], 'L1_attn_Wproj': _L1_attn_in['Wproj'], 'L1_attn_bproj': _L1_attn_in['bproj'], 'L1_ffn_W1': _L1_ffn_in['W1'], 'L1_ffn_b1': _L1_ffn_in['b1'], 'L1_ffn_W2': _L1_ffn_in['W2'], 'L1_ffn_b2': _L1_ffn_in['b2'], 'L1_ffn_Wr1': _L1_ffn_in['Wr1'], 'L1_ffn_br1': _L1_ffn_in['br1'], 'L1_ffn_Wr2': _L1_ffn_in['Wr2'], 'L1_ffn_br2': _L1_ffn_in['br2']}

def reference(x, mask_BS_i1_0, L0_tok_emb_word, L0_tok_emb_pos, L0_tok_emb_ln_s, L0_tok_emb_ln_b, L0_tok_Wq, L0_tok_bq, L0_tok_Wk, L0_tok_bk, L0_tok_Wv, L0_tok_bv, L0_tok_Wo, L0_tok_bo, L0_tok_ln1_s, L0_tok_ln1_b, L0_tok_W1, L0_tok_b1, L0_tok_W2, L0_tok_b2, L0_tok_ln2_s, L0_tok_ln2_b, L0_attn_W_qkv, L0_attn_W_proj, L0_attn_b_proj, L0_attn_temp, L0_ffn_Wg, L0_ffn_bg, L0_ffn_W1, L0_ffn_b1, L0_ffn_W2, L0_ffn_b2, L1_attn_Wqkv, L1_attn_Wproj, L1_attn_bproj, L1_ffn_W1, L1_ffn_b1, L1_ffn_W2, L1_ffn_b2, L1_ffn_Wr1, L1_ffn_br1, L1_ffn_Wr2, L1_ffn_br2):
    import jax
    import jax.numpy as jnp

    def _L0_tok_ref(input_ids, attention_mask, emb_word, emb_pos, emb_ln_s, emb_ln_b, Wq, bq, Wk, bk, Wv, bv, Wo, bo, ln1_s, ln1_b, W1, b1, W2, b2, ln2_s, ln2_b):
        import jax, jax.numpy as jnp
        import numpy as np
        NH = 12
        W = 64
        EPS = 1e-12

        def layer_norm(x, s, b):
            mu = x.mean(-1, keepdims=True)
            var = ((x - mu) ** 2).mean(-1, keepdims=True)
            return (x - mu) / jnp.sqrt(var + EPS) * s + b

        def band_attention(q, k, v, mask):
            B, H, S, d = q.shape
            nc = S // W
            kp = jnp.pad(k, ((0, 0), (0, 0), (W, W), (0, 0)))
            vp = jnp.pad(v, ((0, 0), (0, 0), (W, W), (0, 0)))
            idx = jnp.arange(nc)[:, None] * W + jnp.arange(3 * W)[None, :]
            kb = kp[:, :, idx]
            vb = vp[:, :, idx]
            qc = q.reshape(B, H, nc, W, d)
            scores = jnp.einsum('bhcqd,bhckd->bhcqk', qc, kb) / jnp.sqrt(jnp.asarray(d, q.dtype))
            rel = jnp.arange(3 * W)[None, :] - W - jnp.arange(W)[:, None]
            band_ok = jnp.abs(rel) <= W
            key_abs = idx - W
            pos_ok = (key_abs >= 0) & (key_abs < S)
            mp = jnp.pad(mask, ((0, 0), (W, W)))
            mb = mp[:, idx] > 0
            allowed = mb[:, None, :, None, :] & pos_ok[None, None, :, None, :] & band_ok[None, None, None, :, :]
            scores = jnp.where(allowed, scores, jnp.asarray(-1000000000.0, scores.dtype))
            probs = jax.nn.softmax(scores, axis=-1)
            out = jnp.einsum('bhcqk,bhckd->bhcqd', probs, vb)
            return out.reshape(B, H, S, d)

        def _forward(input_ids, attention_mask, emb_word, emb_pos, emb_ln_s, emb_ln_b, Wq, bq, Wk, bk, Wv, bv, Wo, bo, ln1_s, ln1_b, W1, b1, W2, b2, ln2_s, ln2_b):
            B, S = input_ids.shape
            Hd = emb_word.shape[1]
            dh = Hd // NH
            mask = attention_mask.astype(emb_word.dtype)
            h = layer_norm(emb_word[input_ids] + emb_pos[:S][None], emb_ln_s, emb_ln_b)
            L = Wq.shape[0]
            for l in range(L):

                def heads(x):
                    return x.reshape(B, S, NH, dh).transpose(0, 2, 1, 3)
                q = heads(h @ Wq[l] + bq[l])
                k = heads(h @ Wk[l] + bk[l])
                v = heads(h @ Wv[l] + bv[l])
                a = band_attention(q, k, v, mask)
                a = a.transpose(0, 2, 1, 3).reshape(B, S, Hd)
                h = layer_norm(h + a @ Wo[l] + bo[l], ln1_s[l], ln1_b[l])
                f = jax.nn.gelu(h @ W1[l] + b1[l], approximate=False)
                h = layer_norm(h + f @ W2[l] + b2[l], ln2_s[l], ln2_b[l])
            return h
        return _forward(input_ids, attention_mask, emb_word, emb_pos, emb_ln_s, emb_ln_b, Wq, bq, Wk, bk, Wv, bv, Wo, bo, ln1_s, ln1_b, W1, b1, W2, b2, ln2_s, ln2_b)

    def _L0_attn_ref(x, W_qkv, W_proj, b_proj, temp):
        import jax, jax.numpy as jnp
        import numpy as np
        B, N, C, H = (8, 1024, 192, 8)
        b, n, c = x.shape
        h = temp.shape[0]
        d = c // h
        qkv = (x @ W_qkv).reshape(b, n, h, d, 3)
        q, k, v = (qkv[..., 0], qkv[..., 1], qkv[..., 2])
        q = q / jnp.linalg.norm(q, axis=1, keepdims=True)
        k = k / jnp.linalg.norm(k, axis=1, keepdims=True)
        attn = jnp.einsum('bnhd,bnhe->bhde', q, k) * temp
        attn = jax.nn.softmax(attn, axis=-1)
        y = jnp.einsum('bhde,bnhe->bnhd', attn, v).reshape(b, n, c)
        return y @ W_proj + b_proj

    def _L0_ffn_ref(x, Wg, bg, W1, b1, W2, b2):
        import jax, jax.numpy as jnp
        import numpy as np
        B, T, E = (2, 256, 192)
        H = 768
        N_EXP = 4
        gate_logits = jnp.einsum('bte,en->btn', x, Wg) + bg
        top = jnp.argmax(gate_logits, axis=-1)
        h = jax.nn.gelu(jnp.einsum('bte,neh->nbth', x, W1) + b1[:, None, None, :], approximate=False)
        y = jnp.einsum('nbth,nhe->nbte', h, W2) + b2[:, None, None, :]
        onehot = jax.nn.one_hot(top, N_EXP, dtype=x.dtype)
        out = jnp.einsum('nbte,btn->bte', y, onehot)
        return out

    def _L1_attn_ref(x, Wqkv, Wproj, bproj):
        import jax, jax.numpy as jnp
        import numpy as np
        HEADS = 12
        DIM = 192
        HEAD_DIM = DIM // HEADS
        SCALE = HEAD_DIM ** (-0.5)
        B, S, _ = x.shape
        qkv = x @ Wqkv
        q, k, v = jnp.split(qkv, 3, axis=-1)

        def split_heads(t):
            return t.reshape(B, S, HEADS, HEAD_DIM).transpose(0, 2, 1, 3)
        q, k, v = (split_heads(q), split_heads(k), split_heads(v))
        attn = jnp.einsum('bhqd,bhkd->bhqk', q, k) * SCALE
        attn = jax.nn.softmax(attn, axis=-1)
        out = jnp.einsum('bhqk,bhkd->bhqd', attn, v)
        out = out.transpose(0, 2, 1, 3).reshape(B, S, DIM)
        return out @ Wproj + bproj

    def _L1_ffn_ref(x, W1, b1, W2, b2, Wr1, br1, Wr2, br2):
        import jax, jax.numpy as jnp
        import numpy as np
        E = 8
        K = 2
        D = 192
        F = 4 * D
        h = jax.nn.relu(jnp.einsum('bsd,hd->bsh', x, Wr1) + br1)
        score = jnp.einsum('bsd,ed->bse', h, Wr2) + br2
        _, idx = jax.lax.top_k(score, K)
        mask = (jax.nn.one_hot(idx, E) > 0).any(axis=-2)
        w = jax.nn.softmax(jnp.where(mask, score, -jnp.inf), axis=-1)
        out = jnp.zeros_like(x)
        for e in range(E):
            mid = jax.nn.relu(jnp.einsum('bsd,fd->bsf', x, W1[e]) + b1[e])
            ye = jnp.einsum('bsf,df->bsd', mid, W2[e]) + b2[e]
            out = out + w[..., e:e + 1] * ye
        return out
    h = _L0_tok_ref(x, mask_BS_i1_0, L0_tok_emb_word, L0_tok_emb_pos, L0_tok_emb_ln_s, L0_tok_emb_ln_b, L0_tok_Wq, L0_tok_bq, L0_tok_Wk, L0_tok_bk, L0_tok_Wv, L0_tok_bv, L0_tok_Wo, L0_tok_bo, L0_tok_ln1_s, L0_tok_ln1_b, L0_tok_W1, L0_tok_b1, L0_tok_W2, L0_tok_b2, L0_tok_ln2_s, L0_tok_ln2_b)
    h = h + _L0_attn_ref(_layernorm(h, axis=-1), L0_attn_W_qkv, L0_attn_W_proj, L0_attn_b_proj, L0_attn_temp)
    h = h + _L0_ffn_ref(_layernorm(h, axis=-1), L0_ffn_Wg, L0_ffn_bg, L0_ffn_W1, L0_ffn_b1, L0_ffn_W2, L0_ffn_b2)
    h = h + _L1_attn_ref(_layernorm(h, axis=-1), L1_attn_Wqkv, L1_attn_Wproj, L1_attn_bproj)
    h = h + _L1_ffn_ref(_layernorm(h, axis=-1), L1_ffn_W1, L1_ffn_b1, L1_ffn_W2, L1_ffn_b2, L1_ffn_Wr1, L1_ffn_br1, L1_ffn_Wr2, L1_ffn_br2)
    return h

_drawn_inputs = setup_inputs


def setup_inputs(seed=0):
    import zlib

    import numpy as np

    out = dict(_drawn_inputs(seed))
    spreads = {'L0_tok_emb_ln_s': (1.0, 0.2),
     'L0_tok_emb_ln_b': (0.0, 0.1),
     'L0_tok_bq': (0.0, 0.8),
     'L0_tok_bk': (0.0, 0.8),
     'L0_tok_bv': (0.0, 0.1),
     'L0_tok_bo': (0.0, 0.1),
     'L0_tok_ln1_s': (1.0, 0.2),
     'L0_tok_ln1_b': (0.0, 0.1),
     'L0_tok_b1': (0.0, 0.1),
     'L0_tok_b2': (0.0, 0.1),
     'L0_tok_ln2_s': (1.0, 0.2),
     'L0_tok_ln2_b': (0.0, 0.1),
     'L0_attn_b_proj': (0.0, 0.1),
     'L0_attn_temp': (1.0, 0.6)}
    factors = {'L0_tok_Wq': 8.0,
     'L0_tok_Wk': 7.497,
     'L0_ffn_b1': 3.975,
     'L1_attn_bproj': 6.015,
     'L1_ffn_b1': 8.0,
     'L1_ffn_b2': 4.962,
     'L1_ffn_br1': 4.428}
    for name, (base, spread) in spreads.items():
        noise = np.random.default_rng([zlib.crc32(name.encode()), seed]).standard_normal(out[name].shape)
        drawn = base * np.exp(spread * noise) if base else spread * noise
        out[name] = jnp.asarray(drawn.astype(out[name].dtype))
    for name, factor in factors.items():
        out[name] = (out[name] * factor).astype(out[name].dtype)
    return out
```

```python
from contextlib import ExitStack

import numpy as np

import concourse.bass as bass
from concourse import mybir

ALU = mybir.AluOpType
ACT = mybir.ActivationFunctionType
F32, F32R = mybir.dt.float32, mybir.dt.float32r
F16, BF16, I32 = mybir.dt.float16, mybir.dt.bfloat16, mybir.dt.int32
U32 = mybir.dt.uint32
AX = mybir.AxisListType

P = 128
B, S, D, FF = 8, 256, 192, 768
NT = B * S // P
NG, GT = 4, 4
GW = GT * P
D2 = D - P
LAYERS, HEADS, DH, WIN = 4, 12, 16, 64
FC = FF // P
VOCAB = 8000
SEG = 960
NEG_IN = -2.0 ** 100
NEG_OUT = -3e38
PAIRS_G = 24
PAIRS = NG * PAIRS_G
PROBS = 6
XC_H, XC_D = 8, 24


class Sig:

    AHEAD = 32

    def __init__(self, ctx, nc, name, per=0, base=None):
        self.sem, self.per = ctx.enter_context(nc.semaphore(name)), per
        self.base = self.AHEAD if base is None else base

    def start(self, eng):
        eng.sem_inc(self.sem, self.base)

    def at(self, turn, n):
        return self.base + turn * self.per + n


class Chain:

    def __init__(self, ctx, nc, eng, name, alone=None):
        self.alone = alone
        self.eng, self.sem, self.n, self.turn, self.stride, self.base = (
            eng, ctx.enter_context(nc.semaphore(name)), 0, 0, 0, 0)

    def mark(self, ins):
        ins.then_inc(self.sem, 1)
        self.n += 1
        return self.n

    def done(self, n):
        self.eng.wait_ge(self.sem, self.base + self.turn * self.stride + n)
        if self.alone:
            self.alone(self.eng)

    def link(self, ins):
        self.done(self.mark(ins))

    def enter(self, turn, stride):
        self.base, self.n, self.turn, self.stride = self.base + self.n, 0, turn, stride

    def round_up(self):
        assert 0 < self.n < self.stride, self.n
        self.done(self.n)
        self.eng.sem_inc(self.sem, self.stride - self.n)

    def leave(self, turns):
        self.base, self.n, self.turn, self.stride = self.base + turns * self.stride, 0, 0, 0


def build_tower(nc, a, out, stop=None):
    ctx = ExitStack()
    with ctx:
        def sb(name, shape, dt=F32):
            return ctx.enter_context(nc.sbuf_tensor(name, shape, dt))

        def sig(name, per=0, base=None):
            return Sig(ctx, nc, name, per, base)

        ident = sb("ident", [P, P])
        lo_rows = sb("lo_rows", [P, 1])
        lo_rows_q = sb("lo_rows_q", [P, 1])
        lo_rows_q4 = sb("neg_quarter", [P, 1])
        pad_keys = sb("pad_keys", [P, 2])
        neg_half = sb("neg_half", [P, 4])
        h = sb("h", [P, NT, 256])
        xn = sb("xn", [P, NT, 256])
        hb = sb("hb", [P, NT, D])
        xx = sb("xx", [P, 3, NT * P], F32R)
        qs = sb("qs", [P, 2, 3, GW], F32R)
        kh = sb("kh", [P, 2, 3, GW], F32R)
        kl = sb("kl", [P, 2, 3, GW], F32R)
        qf = sb("qf", [P, 2, GW])
        vf = sb("vf", [P, 4, D])
        vr = sb("vr", [P, 2, D])
        v3 = sb("v3", [P, 2, GT, HEADS, 3, DH], BF16)
        prob = sb("prob", [P, 2, PROBS, 2 * P])
        pth = sb("pth", [P, 3, 4 * P], F16)
        ptl = sb("ptl", [P, 2, 4 * P], F16)
        mask = sb("mask", [P, NT, D], BF16)
        neg_max = sb("neg_max", [P, 2, HEADS])
        row_sum = sb("row_sum", [P, 2, HEADS])
        pad_exp = sb("pad_exp", [P, 2, HEADS])
        rs2 = sb("rs2", [P, 2, HEADS])
        au = sb("au", [P, HEADS, DH])
        stats = sb("stats", [P, NT, 6])
        mv = sb("mv", [P, NT, 2])
        rstd = sb("rstd", [P, NT, 2])
        raw = sb("raw", [P, 2, SEG])
        wa = [sb(f"wa_{n}", [P, SEG], F32R) for n in ("hi", "lo", "second", "second_lo")]
        wb = [sb(f"wb_{n}", [P, SEG], F32R) for n in ("hi", "lo", "second", "second_lo")]
        w2 = [sb(f"w2_{j}", [P, FC, D]) for j in range(2)]
        fbuf = sb("fbuf", [P, 4, GW])
        bqk = sb("bqk", [P, 6])
        b1 = [sb(f"b1_{j}", [P, FC]) for j in range(2)]
        row_bv, row_bo = sb("row_bv", [P, D]), sb("row_bo", [P, D])
        row_b2 = [sb(f"row_b2_{j}", [P, D]) for j in range(2)]
        ln_s, ln_b = sb("ln_s", [P, 2, D]), sb("ln_b", [P, 2, D])
        tok = sb("tok", [P, NT], I32)
        tokf = qf[:, 0, 0:2 * NT].rearrange("p (a n) -> p a n", a=2)
        toku = sb("toku", [P, NT], U32)
        xc_temp = sb("xc_temp", [P, 2])
        room = v3[:, :, :, :, :, :].rearrange("p a b c d e -> p (a b c d e)").bitcast(F32)

        def over(n, *dims):
            nonlocal room
            got, room = room[:, 0:n], room[:, n:]
            return got.rearrange(*dims[:1], **dims[1]) if dims else got

        xc_mask = over(2 * 96, "p (s n) -> p s n", dict(s=2))
        xc_wp = over(2 * D, "p (s n) -> p s n", dict(s=2))
        xc_one = over(96)
        xc_nh = over(4)
        xc_norm = over(2 * 4, "p (s n) -> p s n", dict(s=2))
        xc_s = over(4 * 96, "p (a s n) -> p a s n", dict(a=2, s=2))
        xc_small = over(8, "p (s n) -> p s n", dict(s=4))
        xc_at = over(2 * 96, "p (s n) -> p s n", dict(s=2))
        prefer = sb("prefer", [P, 8])
        gt = [qf[:, 0, j * 8 * NT:(j + 1) * 8 * NT].rearrange("p (t n) -> p t n", n=8) for j in range(3)]
        gm = [qf[:, 0, (24 + j) * NT:(25 + j) * NT] for j in range(3)]
        gate = qf[:, 1, 0:8 * NT].rearrange("p (t n) -> p t n", n=8)
        row_bg, row_br2 = sb("row_bg", [P, 4]), sb("row_br2", [P, 8])
        br1 = sb("br1", [P, 2])
        wr2 = sb("wr2", [P, 2, 8])

        bank = [ctx.enter_context(nc.psum_tensor(f"bank{i}", [P, 512], F32)) for i in range(8)]
        BX, BS, BM, BT, BV, BU, BY = [0, 1], [0, 1, 2], [3, 4, 5], [4, 5], [6, 7], [2, 3], [4, 5, 6, 7]
        BO = [2, 3, 4, 5]

        L = LAYERS
        const_in = sig("const_in", base=0)
        tok_in = sig("tok_in", base=0)
        gathered = sig("gathered", base=0)
        tok_ok = sig("tok_ok", base=0)
        zeroed = sig("zeroed", base=0)
        mask_in, mask_ok = sig("mask_in", base=0), sig("mask_ok", base=0)
        rows_x = sig("rows_x", per=16 * 3, base=0)
        rows_bo = sig("rows_bo", per=16, base=0)
        rows_y = sig("rows_y", per=16 * 8, base=0)
        wa_ready, wb_ready = sig("wa_ready", per=1, base=0), sig("wb_ready", per=1, base=0)
        h_ready = sig("h_ready", per=2 * NT, base=NT)
        hb_ready = sig("hb_ready", per=2 * NT, base=NT)
        mv_ready = sig("mv_ready", per=2 * NG, base=NG)
        rstd_ready = sig("rstd_ready", per=2 * NG, base=NG)
        xt_done = sig("xt_done", per=3 * NT)
        xh_ready = sig("xh_ready", per=3 * NT)
        xx_ready = sig("xx_ready", per=3 * NT)
        proj_done = sig("proj_done", per=10 * NG)
        qf_ready = sig("qf_ready", per=6 * NG)
        qk_ready = sig("qk_ready", per=6 * NG)
        vf_ready = sig("vf_ready", per=4 * NG)
        v3_ready = sig("v3_ready", per=4 * NG)
        s_done = sig("s_done", per=2 * PAIRS)
        max_ready = sig("max_ready", per=2 * PAIRS)
        exp_done = sig("exp_done", per=2 * PAIRS)
        pad_ready = sig("pad_ready", per=NT)
        t_done = sig("t_done", per=PAIRS)
        hi_ready, lo_ready = sig("hi_ready", per=PAIRS), sig("lo_ready", per=PAIRS)
        pv_done = sig("pv_done", per=PAIRS)
        att_ready = sig("att_ready", per=NT)
        o_done = sig("o_done", per=NT)
        o_read = sig("o_read", per=NT)
        u_done = sig("u_done", per=NG * FC)
        f_ready = sig("f_ready", per=NG * FC)
        y_done = sig("y_done", per=NG * FC)
        y_read = sig("y_read", per=NT)
        out_done = sig("out_done", base=0)
        passed = {nc.vector.engine: sig("vector_passed", base=0), nc.gpsimd.engine: sig("pool_passed", base=0)}
        tok_hidden = (u_done, f_ready, y_done, y_read)
        xn_ready = sig("xn_ready")
        xc_qk_done, xc_v_done = sig("xc_qk_done"), sig("xc_v_done")
        xc_qk_ready, xc_v_ready = sig("xc_qk_ready"), sig("xc_v_ready")
        xc_gram_done, xc_norm_ready, xc_pow_ready = sig("xc_gram_done"), sig("xc_norm_ready"), sig("xc_pow_ready")
        xc_s_ready, xc_e_ready, xc_p_ready = sig("xc_s_ready"), sig("xc_e_ready"), sig("xc_p_ready")
        xc_k_ready, xc_kt_done = sig("xc_k_ready"), sig("xc_kt_done")
        xc_pt_done, xc_pt_ready = sig("xc_pt_done"), sig("xc_pt_ready")
        xc_y_done, xc_y_ready = sig("xc_y_done"), sig("xc_y_ready")
        xc_o_done, xc_o_ready = sig("xc_o_done"), sig("xc_o_ready")
        gates_done, gates_ready = sig("gates_done"), sig("gates_ready")
        r_done, r_ready = sig("router_hidden_done"), sig("router_hidden_ready")
        g2_done, g2_max, g2_exp = sig("router_done"), sig("router_max"), sig("router_exp")
        aux_in = sig("aux_in", base=0)
        seg_q_in, seg_q_ready = sig("att1_segment_in", base=0), sig("att1_segment_ready")
        sum_ready = sig("sum_ready")
        moe = []
        for m, name in enumerate(("moe0", "moe1")):
            moe.append(dict(
                hidden=(sig(name + "_u_done", per=NG * FC), sig(name + "_f_ready", per=NG * FC),
                        sig(name + "_y_done", per=NG * FC), sig(name + "_y_read", per=NT)),
                seg_in=sig(name + "_segment_in", per=16 * 4, base=0),
                seg_ready=sig(name + "_segment_ready", per=1)))

        block = ctx.enter_context(nc.Block())

        def alone(eng):
            eng.sem_inc(passed[eng.engine].sem, 1)

        def pe_transpose(pe, it, k, t, src, ready, turn, n):
            pe.wait_ge(ready.sem, ready.at(turn, n))
            pe.wait_ge(xx_ready.sem, xx_ready.at(it, k * NT + t - 1))
            for c in range(2):
                last = nc.tensor.transpose(bank[BX[t % 2]][:, c * P:c * P + P],
                                           src[:, t, c * P:c * P + P], ident[:, :])
            last.then_inc(xt_done.sem, 1)

        def pe_features(o, w, c0, g):
            tk, c = slice(g * GW, g * GW + GW), slice(c0, c0 + P)
            hi, lo, second, second_lo = w
            nc.tensor.matmul(o, hi[:, c], xx[:, 0, tk], start=True, stop=False)
            nc.tensor.matmul(o, hi[:, c], xx[:, 2, tk], start=False, stop=False)
            nc.tensor.matmul(o, lo[:, c], xx[:, 0, tk], start=False, stop=False)
            nc.tensor.matmul(o, second[:, c], xx[:, 1, tk], start=False, stop=False)
            return nc.tensor.matmul(o, second_lo[0:D2, c], xx[0:D2, 1, tk], start=False, stop=True)

        def pe_tokens(o, w, c0, n, t):
            tk, c = slice(t * P, t * P + P), slice(c0, c0 + n)
            hi, lo, second, second_lo = w
            nc.tensor.matmul(o, xx[:, 0, tk], hi[:, c], start=True, stop=False)
            nc.tensor.matmul(o, xx[:, 0, tk], lo[:, c], start=False, stop=False)
            nc.tensor.matmul(o, xx[:, 2, tk], hi[:, c], start=False, stop=False)
            nc.tensor.matmul(o, xx[:, 1, tk], second[:, c], start=False, stop=False)
            return nc.tensor.matmul(o, xx[0:D2, 1, tk], second_lo[0:D2, c], start=False, stop=True)

        def projection_at(g, i):
            return bank[BM[i % 3 if g == 0 else 0]]

        def pe_qkv(pe, it, g, i, wa):
            n = 10 * g + i
            proj_read(pe, it, n - (3 if g == 0 else 1))
            o = projection_at(g, i)
            if i < 6:
                last = pe_features(o[:, :], wa, i * P, g)
            else:
                last = pe_tokens(o[:, 0:D], wa, FF, D, GT * g + i - 6)
            last.then_inc(proj_done.sem, 1)

        def proj_read(pe, it, n):
            g, i = n // 10, n % 10
            if n < 0:
                return
            if i < 6:
                pe.wait_ge(qk_ready.sem, qk_ready.at(it, 6 * g + i + 1))
            else:
                pe.wait_ge(vf_ready.sem, vf_ready.at(it, 4 * g + i - 6 + 1))

        def where(u):
            return u // (2 * HEADS), u // HEADS % 2, u % HEADS

        def keys(qt, banded):
            return slice(qt * WIN, qt * WIN + D) if banded else slice(0, S)

        def scores_at(u, n):
            return bank[BS[u % 3]][:, 0:n]

        def beside(tile, xx=None):
            steps = {i: (lambda i=i: (tile(GT + 2 * i), tile(GT + 2 * i + 1))) for i in range((NT - GT) // 2)}
            steps["xx"] = xx
            return steps

        def next_projection(p):
            g, k = p // PAIRS_G + 1, p % PAIRS_G
            if g < NG and k % 2 == 1 and k < 20:
                return g, k // 2
            return None

        def pe_scores(pe, it, u, banded):
            b, qt, hd = where(u)
            g, r, s0 = b // 2, 32 * (hd % 4), (b % 2) * S
            pe.wait_ge(exp_done.sem, exp_done.at(it, u - 2))
            pe.wait_ge(qk_ready.sem, qk_ready.at(it, 6 * g + 6))
            ks = keys(qt, banded)
            q = qs[r:r + 32, g % 2, hd // 4, s0 + qt * P:s0 + qt * P + P]
            o = scores_at(u, ks.stop - ks.start)
            nc.tensor.matmul(o, q, kh[r:r + 32, g % 2, hd // 4, s0 + ks.start:s0 + ks.stop],
                             start=True, stop=False)
            nc.tensor.matmul(o, q, kl[r:r + 32, g % 2, hd // 4, s0 + ks.start:s0 + ks.stop],
                             start=False, stop=True).then_inc(s_done.sem, 1)

        def pe_turn_probs(pe, it, p):
            pe.wait_ge(exp_done.sem, exp_done.at(it, 2 * p + 2))
            pe.wait_ge(lo_ready.sem, lo_ready.at(it, p - 1))
            for e in range(2):
                _, qt, hd = where(2 * p + e)
                for c in range(2):
                    last = nc.tensor.transpose(bank[BT[p % 2]][:, (2 * e + c) * P:(2 * e + c) * P + P],
                                               prob[:, qt, hd % PROBS, c * P:c * P + P], ident[:, :])
            last.then_inc(t_done.sem, 1)

        def pe_values(pe, it, p):
            b, qt, _ = where(2 * p)
            pe.wait_ge(lo_ready.sem, lo_ready.at(it, p + 1))
            pe.wait_ge(v3_ready.sem, v3_ready.at(it, 4 * (b // 2) + 2 * (b % 2) + 2))
            if p % 6 == 0:
                pe.wait_ge(att_ready.sem, att_ready.at(it, 2 * b + qt - 1))
            for e in range(2):
                hd = (2 * p + e) % HEADS
                o = bank[BV[qt]]
                for c in range(2):
                    w = slice((2 * e + c) * P, (2 * e + c) * P + P)
                    v = v3[:, (b // 2) % 2, 2 * (b % 2) + c, hd, :, :].rearrange("p a d -> p (a d)")
                    o2, o1 = o[:, hd * 32:hd * 32 + 32], o[:, hd * 32 + DH:hd * 32 + 32]
                    nc.tensor.matmul(o2, pth[:, p % 3, w], v[:, 0:32], start=(c == 0), stop=False)
                    nc.tensor.matmul(o1, pth[:, p % 3, w], v[:, 32:48], start=False, stop=False)
                    last = nc.tensor.matmul(o2, ptl[:, p % 2, w], v[:, 0:32], start=False, stop=(c == 1))
            last.then_inc(pv_done.sem, 1)

        def pe_attention(pe, it, banded, w, before):
            for i in range(10):
                pe_qkv(pe, it, 0, i, w)
                if i in before:
                    before[i]()
            pe.wait_ge(xx_ready.sem, xx_ready.at(*before["xx"](NT)))
            for p in range(PAIRS + 4):
                if p < PAIRS:
                    pe_scores(pe, it, 2 * p, banded)
                    pe_scores(pe, it, 2 * p + 1, banded)
                if p >= 4:
                    pe_values(pe, it, p - 4)
                if p == 2:
                    pe.wait_ge(vf_ready.sem, vf_ready.at(it, 4))
                if 0 <= p - 2 < PAIRS:
                    pe_turn_probs(pe, it, p - 2)
                if next_projection(p):
                    g, i = next_projection(p)
                    pe_qkv(pe, it, g, i, w)

        def pe_out(pe, it, w, c0, g, xt):
            for t in range(GT * g, GT * g + GT):
                pe.wait_ge(xx_ready.sem, xx_ready.at(*xt(t)))
                pe.wait_ge(o_read.sem, o_read.at(it, t - 3))
                pe_tokens(bank[BO[t % 4]][:, 0:D], w, c0, D, t).then_inc(o_done.sem, 1)

        def pe_hidden(pe, it, k, w, w2, sigs, before):
            u_done, f_ready, y_done, y_read = sigs
            for n in range(NG * FC + 2):
                if n in before:
                    before[n]()
                if n < NG * FC:
                    g, c = n // FC, n % FC
                    if c == 0 and k is not None:
                        pe.wait_ge(xx_ready.sem, xx_ready.at(it, k * NT + GT * (g + 1)))
                    pe.wait_ge(f_ready.sem, f_ready.at(it, n - 1))
                    pe_features(bank[BU[n % 2]][:, :], w, D + c * P, g).then_inc(u_done.sem, 1)
                if n >= 2:
                    g, c = (n - 2) // FC, (n - 2) % FC
                    pe.wait_ge(f_ready.sem, f_ready.at(it, n - 1))
                    for t in range(GT):
                        if c == 0:
                            pe.wait_ge(y_read.sem, y_read.at(it, GT * (g - 1) + t + 1))
                        last = nc.tensor.matmul(bank[BY[t]][:, 0:D], fbuf[:, (n - 2) % 4, t * P:t * P + P],
                                                w2[:, c, :], start=(c == 0), stop=(c == FC - 1))
                    last.then_inc(y_done.sem, 1)

        def act_split(act, it, k, t):
            act.wait_ge(xt_done.sem, xt_done.at(it, k * NT + t + 1))
            nc.scalar.activation(xx[:, 0:2, t * P:t * P + P],
                                 bank[BX[t % 2]][:, 0:2 * P].rearrange("p (a n) -> p a n", a=2),
                                 ACT.Copy).then_inc(xh_ready.sem, 1)

        def act_qk(act, it, g, i, banded):
            n = 6 * g + i
            act.wait_ge(proj_done.sem, proj_done.at(it, 10 * g + i + 1))
            act.wait_ge(qk_ready.sem, qk_ready.at(it, n - 1))
            o, s = projection_at(g, i)[:, :], i % 3
            hi = qs[:, g % 2, s, :] if i < 3 else kh[:, g % 2, s, :]
            if banded:
                nc.scalar.activation(qf[:, n % 2, :], o, ACT.Identity, bias=bqk[:, i:i + 1])
                nc.scalar.activation(hi, o, ACT.Identity, bias=bqk[:, i:i + 1]).then_inc(qf_ready.sem, 1)
            else:
                sc = DH ** -0.5 if i < 3 else 1.0
                nc.scalar.activation(qf[:, n % 2, :], o, ACT.Copy, scale=sc)
                nc.scalar.activation(hi, o, ACT.Copy, scale=sc).then_inc(qf_ready.sem, 1)

        def act_exp(act, it, u, banded):
            b, qt, hd = where(u)
            tile_no = 2 * b + qt
            act.wait_ge(max_ready.sem, max_ready.at(it, u + 1))
            back = u - PROBS if hd >= PROBS else u - 2 * HEADS + PROBS
            if back >= 0:
                act.wait_ge(t_done.sem, t_done.at(it, back // 2 + 1))
            if hd == 0:
                act.wait_ge(att_ready.sem, att_ready.at(it, tile_no - 1))
            n = D if banded else S
            c0 = keys(qt, banded).start
            nc.scalar.activation(prob[:, qt, hd % PROBS, c0:c0 + n], scores_at(u, n), ACT.Exp,
                                 bias=neg_max[:, tile_no % 2, hd:hd + 1], scale=-1.0 if banded else 1.0,
                                 accum_out=row_sum[:, tile_no % 2, hd:hd + 1]).then_inc(exp_done.sem, 1)
            if hd == HEADS - 1 and banded:
                nc.scalar.activation(pad_exp[:, tile_no % 2, :], neg_max[:, tile_no % 2, :], ACT.Exp,
                                     bias=lo_rows_q4[:, :]).then_inc(pad_ready.sem, 1)

        def act_hi(act, it, p):
            act.wait_ge(t_done.sem, t_done.at(it, p + 1))
            act.wait_ge(pv_done.sem, pv_done.at(it, p - 2))
            nc.scalar.activation(pth[:, p % 3, :], bank[BT[p % 2]][:, :], ACT.Copy).then_inc(hi_ready.sem, 1)

        def act_attention(act, it, banded, split):
            for i in range(10):
                if i < 6:
                    act_qk(act, it, 0, i, banded)
                if i in split:
                    split[i]()
            for p in range(PAIRS + 2):
                if p < PAIRS:
                    act_exp(act, it, 2 * p, banded)
                if 0 <= p - 2 < PAIRS:
                    act_hi(act, it, p - 2)
                if p < PAIRS:
                    act_exp(act, it, 2 * p + 1, banded)
                if next_projection(p):
                    g, i = next_projection(p)
                    if i < 6:
                        act_qk(act, it, g, i, banded)

        def act_hidden(act, it, k, b1, sigs, func):
            u_done, f_ready, y_done, y_read = sigs
            if k is not None:
                for t in range(3 * GT):
                    act_split(act, it, k, t)
            for n in range(NG * FC):
                if n == 2 and k is not None:
                    for t in range(3 * GT, NT):
                        act_split(act, it, k, t)
                act.wait_ge(u_done.sem, u_done.at(it, n + 1))
                act.wait_ge(y_done.sem, y_done.at(it, n - 3))
                nc.scalar.activation(fbuf[:, n % 4, :], bank[BU[n % 2]][:, :], func,
                                     bias=b1[:, n % FC:n % FC + 1]).then_inc(f_ready.sem, 1)

        def dve_split(dve, it, k, t):
            dve.wait_ge(xh_ready.sem, xh_ready.at(it, k * NT + t + 1))
            ps, tk = bank[BX[t % 2]], slice(t * P, t * P + P)
            nc.vector.tensor_tensor(xx[:, 2, tk], ps[:, 0:P], xx[:, 0, tk].bitcast(F32), ALU.subtract)
            nc.vector.scalar_tensor_tensor(xx[:, 1, tk], in0=xx[:, 1, tk].bitcast(F32), scalar=lo_rows[:, :],
                                           in1=ps[:, P:2 * P], op0=ALU.mult, op1=ALU.add)\
                .then_inc(xx_ready.sem, 1)

        def dve_qk(dve, it, g, i):
            n, s = 6 * g + i, i % 3
            dve.wait_ge(qf_ready.sem, qf_ready.at(it, n + 1))
            if i < 3:
                q = qs[:, g % 2, s, :]
                nc.vector.scalar_tensor_tensor(q, in0=q.bitcast(F32), scalar=lo_rows_q[:, :],
                                               in1=qf[:, n % 2, :], op0=ALU.mult, op1=ALU.add)\
                    .then_inc(qk_ready.sem, 1)
            else:
                nc.vector.tensor_tensor(kl[:, g % 2, s, :], qf[:, n % 2, :],
                                        kh[:, g % 2, s, :].bitcast(F32), ALU.subtract)\
                    .then_inc(qk_ready.sem, 1)

        def dve_v(dve, it, g, i, banded):
            n = 4 * g + i
            dve.wait_ge(proj_done.sem, proj_done.at(it, 10 * g + 6 + i + 1))
            dve.wait_ge(v3_ready.sem, v3_ready.at(it, n - 3))
            o = projection_at(g, 6 + i)[:, 0:D]
            if banded:
                nc.vector.tensor_tensor(vf[:, i, :], o, row_bv[:, :], ALU.add).then_inc(vf_ready.sem, 1)
            else:
                nc.vector.tensor_copy(vf[:, i, :], o).then_inc(vf_ready.sem, 1)

        def dve_max(dve, it, u, banded):
            b, qt, hd = where(u)
            t = 2 * b + qt
            dve.wait_ge(s_done.sem, s_done.at(it, u + 1))
            if banded:
                alone(dve)
            m = neg_max[:, t % 2, hd:hd + 1]
            if banded:
                nc.vector.tensor_tensor_reduce(out=scores_at(u, D), in0=scores_at(u, D), in1=mask[:, t, :],
                                               scale=-(DH ** -0.5), scalar=3e38, op0=ALU.add, op1=ALU.min,
                                               accum_out=m).then_inc(max_ready.sem, 1)
            else:
                nc.vector.tensor_reduce(m, scores_at(u, S), AX.X, ALU.max, negate=True).then_inc(max_ready.sem, 1)

        def dve_lo(dve, it, p):
            dve.wait_ge(hi_ready.sem, hi_ready.at(it, p + 1))
            dve.wait_ge(pv_done.sem, pv_done.at(it, p - 1))
            nc.vector.tensor_tensor(ptl[:, p % 2, :], bank[BT[p % 2]][:, :], pth[:, p % 3, :], ALU.subtract)\
                .then_inc(lo_ready.sem, 1)

        def dve_finish(dve, ch, it, t, banded):
            dve.wait_ge(pv_done.sem, pv_done.at(it, 6 * t + 6))
            ps = bank[BV[t % 2]][:, 0:2 * D].rearrange("p (h a d) -> p h d a", a=2, d=DH)
            if banded:
                dve.wait_ge(pad_ready.sem, pad_ready.at(it, t + 1))
                c = ch.mark(nc.vector.scalar_tensor_tensor(
                    rs2[:, 0, :], in0=pad_exp[:, t % 2, :], scalar=pad_keys[:, t % 2:t % 2 + 1],
                    in1=row_sum[:, t % 2, :], op0=ALU.mult, op1=ALU.add))
                src = rs2[:, 0, :]
            else:
                c, src = None, row_sum[:, t % 2, :]
            c2 = ch.mark(nc.vector.tensor_reduce(au[:, :, :], ps, AX.X, ALU.add))
            if c:
                ch.done(c)
            ch.mark(nc.vector.reciprocal(rs2[:, 1, :], src))
            ch.done(c2 + 1)
            r = rs2[:, 1, :].unsqueeze(2).to_broadcast([P, HEADS, DH])
            o = xn[:, t, :].rearrange("p (h d) -> p h d", d=DH)
            nc.vector.tensor_tensor(o[:, 0:HEADS, :], au[:, :, :], r, ALU.mult)
            nc.vector.tensor_tensor(o[:, HEADS:, :], au[:, 8:HEADS, :], r[:, 8:HEADS, :], ALU.mult)\
                .then_inc(att_ready.sem, 1)

        def dve_attention(dve, ch, it, banded, split):
            for i in range(10):
                if i < 6:
                    dve_qk(dve, it, 0, i)
                else:
                    dve_v(dve, it, 0, i - 6, banded)
                if i in split:
                    split[i]()
            for p in range(PAIRS + 6):
                if p < PAIRS:
                    dve_max(dve, it, 2 * p, banded)
                if 0 <= p - 3 < PAIRS:
                    dve_lo(dve, it, p - 3)
                if p < PAIRS:
                    dve_max(dve, it, 2 * p + 1, banded)
                if p and next_projection(p - 1):
                    g, i = next_projection(p - 1)
                    if i < 6:
                        dve_qk(dve, it, g, i)
                    else:
                        dve_v(dve, it, g, i - 6, banded)
                if p >= 5 and (p - 5) % 6 == 5:
                    dve_finish(dve, ch, it, (p - 5) // 6, banded)

        def dve_residual(dve, ch, it, half, g, hb_n=None):
            for t in range(GT * g, GT * g + GT):
                dve.wait_ge(hb_ready.sem, hb_ready.at(it, (half - 1) * NT + t + 1 if hb_n is None else hb_n + t))
                if half == 0:
                    dve.wait_ge(o_done.sem, o_done.at(it, t + 1))
                    ps, read = bank[BO[t % 4]], o_read
                else:
                    dve.wait_ge(y_done.sem, y_done.at(it, FC * (g + 1)))
                    ps, read = bank[BY[t % 4]], y_read
                nc.vector.tensor_tensor(h[:, t, 0:D], ps[:, 0:D], hb[:, t, :], ALU.add)\
                    .then_inc(read.sem, 1)

        def dve_stats(dve, ch, it, half, g, read):
            c = []
            for i in range(GT):
                if read:
                    dve.wait_ge(read.sem, read.at(it, GT * g + i + 1))
                c.append(ch.mark(nc.vector.bn_stats(stats[:, GT * g + i, :], h[:, GT * g + i, 0:D])))
            for i in range(GT):
                ch.done(c[i])
                alone(dve)
                last = nc.vector.bn_aggr(mv[:, GT * g + i, :], stats[:, GT * g + i, :])
                if i < GT - 1:
                    ch.mark(last)
            last.then_inc(mv_ready.sem, 1)

        def dve_normalise(dve, ch, it, n, g):
            dve.wait_ge(rstd_ready.sem, rstd_ready.at(it, n))
            for t in range(GT * g, GT * g + GT):
                for dst, src in ((slice(0, D), slice(0, D)), (slice(D, 256), slice(P, D))):
                    last = nc.vector.tensor_scalar(xn[:, t, dst], h[:, t, src], mv[:, t, 0:1],
                                                   rstd[:, t, 1:2], ALU.subtract, ALU.mult)
                last.then_inc(xn_ready.sem, 1)

        def dve_norm_in(dve, ch, it, half, turn):
            for g in range(NG + 1):
                if g < NG:
                    dve_stats(dve, ch, it, half, g, None)
                if g:
                    dve_normalise(dve, ch, it, half * NG + g, g - 1)
            if turn is not None:
                for t in range(NT):
                    dve_split(dve, it, turn, t)

        def dve_affine(dve, ch, it, half, g, w):
            dve.wait_ge(rstd_ready.sem, rstd_ready.at(it, NG * (half - 1) + g + 1))
            c = []
            for t in range(GT * g, GT * g + GT):
                c.append(ch.mark(nc.vector.scalar_tensor_tensor(
                    h[:, t, 0:D], in0=h[:, t, 0:D], scalar=mv[:, t, 0:1], in1=ln_s[:, w, :],
                    op0=ALU.subtract, op1=ALU.mult)))
            for i, t in enumerate(range(GT * g, GT * g + GT)):
                ch.done(c[i])
                c[i] = ch.mark(nc.vector.scalar_tensor_tensor(
                    h[:, t, 0:D], in0=h[:, t, 0:D], scalar=rstd[:, t, 1:2], in1=ln_b[:, w, :],
                    op0=ALU.mult, op1=ALU.add))
            for i, t in enumerate(range(GT * g, GT * g + GT)):
                ch.done(c[i])
                nc.vector.tensor_copy(h[:, t, D:], h[:, t, P:D]).then_inc(h_ready.sem, 1)

        def pool_rstd(pool, ch, it, n, g, eps):
            pool.wait_ge(mv_ready.sem, mv_ready.at(it, n))
            alone(pool)
            t = slice(GT * g, GT * g + GT)
            ch.link(nc.gpsimd.tensor_scalar(rstd[:, t, 0], mv[:, t, 1], eps, None, ALU.add))
            nc.gpsimd.tensor_tensor(rstd[:, t, 1], rstd[:, t, 0], neg_half[:, :], ALU.pow)\
                .then_inc(rstd_ready.sem, 1)

        def pool_hb(pool, it, n0, g, row):
            for t in range(GT * g, GT * g + GT):
                pool.wait_ge(h_ready.sem, h_ready.at(it, n0 + t + 1))
                nc.gpsimd.tensor_tensor(hb[:, t, :], h[:, t, 0:D], row[:, :], ALU.add)\
                    .then_inc(hb_ready.sem, 1)

        def pool_weights(ch, w, c1):
            hi, lo, second, second_lo = w
            ch.mark(nc.gpsimd.tensor_copy(hi[:, 0:c1], raw[:, 0, 0:c1]))
            c = ch.mark(nc.gpsimd.tensor_copy(second[:, 0:c1], raw[:, 1, 0:c1]))
            ch.done(c)
            nc.gpsimd.tensor_tensor(lo[:, 0:c1], raw[:, 0, 0:c1], hi[:, 0:c1].bitcast(F32), ALU.subtract)
            return nc.gpsimd.tensor_tensor(second_lo[0:D2, 0:c1], raw[0:D2, 1, 0:c1],
                                           second[0:D2, 0:c1].bitcast(F32), ALU.subtract)

        def pool_v(pool, ch, it, g):
            for i in range(4):
                n = 4 * g + i
                pool.wait_ge(vf_ready.sem, vf_ready.at(it, n + 1))
                if i == 0:
                    pool.wait_ge(pv_done.sem, pv_done.at(it, PAIRS_G * (g - 1)))
                alone(pool)
                v = [v3[:, g % 2, i, :, a, :] for a in range(3)]
                x = vf[:, i, :].rearrange("p (h d) -> p h d", d=DH)
                r = [vr[:, a, :].rearrange("p (h d) -> p h d", d=DH) for a in range(2)]
                ch.link(nc.gpsimd.tensor_copy(v[0], x))
                ch.link(nc.gpsimd.tensor_tensor(r[0], x, v[0], ALU.subtract))
                ch.link(nc.gpsimd.tensor_copy(v[1], r[0]))
                nc.gpsimd.tensor_tensor(v[2], r[0], v[1], ALU.subtract).then_inc(v3_ready.sem, 1)
                pool.wait_ge(v3_ready.sem, v3_ready.at(it, n + 1))

        NB = B
        qkt = lambda b, i: fbuf[:, 2 * (b % 2) + i, 0:2 * D]
        sqt = lambda i: qf[:, i, 0:2 * D]
        vt = lambda b: prob[0:96, b % 2, 0:2, :]
        yt = lambda b: prob[0:96, b % 2, 2:4, :]

        def pe_xc_front(pe, b):
            for i in range(2):
                t = 2 * b + i
                pe.wait_ge(xc_qk_ready.sem, xc_qk_ready.at(0, 2 * (b - 1) + i + 1))
                pe_tokens(bank[3 + i][:, 0:2 * D], wa, 0, 2 * D, t).then_inc(xc_qk_done.sem, 1)
            pe.wait_ge(xc_v_ready.sem, xc_v_ready.at(0, b))
            for s in range(2):
                tk, c = slice(b * S, b * S + S), slice(2 * D + 96 * s, 2 * D + 96 * s + 96)
                o = bank[5][0:96, s * S:s * S + S]
                hi, lo, second, second_lo = wa
                nc.tensor.matmul(o, hi[:, c], xx[:, 0, tk], start=True, stop=False)
                nc.tensor.matmul(o, hi[:, c], xx[:, 2, tk], start=False, stop=False)
                nc.tensor.matmul(o, lo[:, c], xx[:, 0, tk], start=False, stop=False)
                nc.tensor.matmul(o, second[:, c], xx[:, 1, tk], start=False, stop=False)
                last = nc.tensor.matmul(o, second_lo[0:D2, c], xx[0:D2, 1, tk], start=False, stop=True)
            last.then_inc(xc_v_done.sem, 1)

        def pe_xc_gram(pe, b):
            pe.wait_ge(xc_qk_ready.sem, xc_qk_ready.at(0, 2 * b + 2))
            pe.wait_ge(xc_norm_ready.sem, xc_norm_ready.at(0, b - 1))
            pe.wait_ge(xc_s_ready.sem, xc_s_ready.at(0, b - 1))
            o = bank[6 + b % 2]
            for s in range(2):
                c = slice(96 * s, 96 * s + 96)
                ck = slice(D + 96 * s, D + 96 * s + 96)
                for i in range(2):
                    nc.tensor.matmul(o[0:96, c], qkt(b, i)[:, ck], qkt(b, i)[:, c], start=(i == 0), stop=(i == 1))
                for at, cols in ((D + s, ck), (D + 2 + s, c)):
                    for i in range(2):
                        last = nc.tensor.matmul(o[0:96, at:at + 1], sqt(i)[:, cols], xc_one[:, 0:1],
                                                start=(i == 0), stop=(i == 1))
            last.then_inc(xc_gram_done.sem, 1)

        def pe_xc_turn(pe, b):
            pe.wait_ge(xc_k_ready.sem, xc_k_ready.at(0, b + 1))
            for s in range(2):
                last = nc.tensor.transpose(bank[6 + b % 2][0:96, 256 + 96 * s:256 + 96 * s + 96],
                                           xc_s[0:96, 1, s, :], ident[0:96, 0:96])
            last.then_inc(xc_kt_done.sem, 1)

        def pe_xc_back(pe, b):
            pe.wait_ge(xc_p_ready.sem, xc_p_ready.at(0, b + 1))
            pe.wait_ge(xc_pt_ready.sem, xc_pt_ready.at(0, b))
            for s in range(2):
                last = nc.tensor.transpose(bank[0][0:96, 96 * s:96 * s + 96], xc_s[0:96, 0, s, :],
                                           ident[0:96, 0:96])
            last.then_inc(xc_pt_done.sem, 1)
            pe.wait_ge(xc_pt_ready.sem, xc_pt_ready.at(0, b + 1))
            pe.wait_ge(xc_v_ready.sem, xc_v_ready.at(0, b + 1))
            pe.wait_ge(xc_y_ready.sem, xc_y_ready.at(0, b))
            for s in range(2):
                last = nc.tensor.matmul(bank[1][0:96, s * S:s * S + S], xc_at[0:96, s, :], vt(b)[:, s, :],
                                        start=True, stop=True)
            last.then_inc(xc_y_done.sem, 1)
            pe.wait_ge(xc_y_ready.sem, xc_y_ready.at(0, b + 1))
            pe.wait_ge(xc_o_ready.sem, xc_o_ready.at(0, 2 * b))
            for i in range(2):
                for s in range(2):
                    last = nc.tensor.matmul(bank[2][:, i * D:i * D + D], yt(b)[:, s, i * P:i * P + P],
                                            xc_wp[0:96, s, :], start=(s == 0), stop=(s == 1))
            last.then_inc(xc_o_done.sem, 1)

        def act_xc_front(act, b):
            for i in range(2):
                act.wait_ge(xc_qk_done.sem, xc_qk_done.at(0, 2 * b + i + 1))
                act.wait_ge(xc_gram_done.sem, xc_gram_done.at(0, b))
                nc.scalar.activation(sqt(i), bank[3 + i][:, 0:2 * D], ACT.Square)
                nc.scalar.activation(qkt(b, i), bank[3 + i][:, 0:2 * D], ACT.Copy).then_inc(xc_qk_ready.sem, 1)
            act.wait_ge(xc_v_done.sem, xc_v_done.at(0, b + 1))
            act.wait_ge(xc_y_done.sem, xc_y_done.at(0, b - 1))
            nc.scalar.activation(vt(b), bank[5][0:96, :].rearrange("p (s n) -> p s n", s=2), ACT.Copy)\
                .then_inc(xc_v_ready.sem, 1)

        def act_xc_exp(act, b):
            act.wait_ge(xc_s_ready.sem, xc_s_ready.at(0, b + 1))
            act.wait_ge(xc_p_ready.sem, xc_p_ready.at(0, b))
            for s in range(2):
                last = nc.scalar.activation(xc_s[0:96, 1, s, :], xc_s[0:96, 0, s, :], ACT.Exp,
                                            bias=xc_small[0:96, 1, s:s + 1],
                                            accum_out=xc_small[0:96, 2, s:s + 1])
            last.then_inc(xc_e_ready.sem, 1)

        def act_xc_back(act, b):
            act.wait_ge(xc_y_done.sem, xc_y_done.at(0, b + 1))
            act.wait_ge(xc_o_done.sem, xc_o_done.at(0, b - 1))
            nc.scalar.activation(yt(b), bank[1][0:96, :].rearrange("p (s n) -> p s n", s=2), ACT.Copy)\
                .then_inc(xc_y_ready.sem, 1)

        def dve_xc_logits(dve, ch, b):
            o = bank[6 + b % 2][0:96, :]
            dve.wait_ge(xc_gram_done.sem, xc_gram_done.at(0, b + 1))
            dve.wait_ge(xc_pow_ready.sem, xc_pow_ready.at(0, b - 1))
            nc.vector.tensor_copy(xc_norm[0:96, 0, :], o[:, D:D + 4]).then_inc(xc_norm_ready.sem, 1)
            dve.wait_ge(xc_pow_ready.sem, xc_pow_ready.at(0, b + 1))
            dve.wait_ge(xc_pt_done.sem, xc_pt_done.at(0, b))
            inv = xc_norm[0:96, 1, :]
            nc.vector.tensor_tensor(xc_s[0:96, 1, :, :], o[:, 0:D].rearrange("p (s n) -> p s n", s=2),
                                    inv[:, 0:2].unsqueeze(2).to_broadcast([96, 2, 96]), ALU.mult)\
                .then_inc(xc_k_ready.sem, 1)
            ch.link(nc.vector.tensor_tensor(xc_small[0:96, 0, :], inv[:, 2:4], xc_temp[0:96, :], ALU.mult))
            dve.wait_ge(xc_kt_done.sem, xc_kt_done.at(0, b + 1))
            ch.link(nc.vector.tensor_tensor(xc_s[0:96, 0, :, :],
                                            o[:, 256:256 + D].rearrange("p (s n) -> p s n", s=2),
                                            xc_small[0:96, 0, :].unsqueeze(2).to_broadcast([96, 2, 96]), ALU.mult))
            ch.link(nc.vector.tensor_tensor(xc_s[0:96, 0, :, :], xc_s[0:96, 0, :, :], xc_mask[0:96, :, :], ALU.add))
            nc.vector.tensor_reduce(xc_small[0:96, 1, :], xc_s[0:96, 0, :, :], AX.X, ALU.max, negate=True)\
                .then_inc(xc_s_ready.sem, 1)

        def dve_xc_probs(dve, ch, b):
            dve.wait_ge(xc_e_ready.sem, xc_e_ready.at(0, b + 1))
            ch.link(nc.vector.reciprocal(xc_small[0:96, 3, :], xc_small[0:96, 2, :]))
            nc.vector.tensor_tensor(xc_s[0:96, 0, :, :], xc_s[0:96, 1, :, :],
                                    xc_small[0:96, 3, :].unsqueeze(2).to_broadcast([96, 2, 96]), ALU.mult)\
                .then_inc(xc_p_ready.sem, 1)
            dve.wait_ge(xc_pt_done.sem, xc_pt_done.at(0, b + 1))
            dve.wait_ge(xc_y_done.sem, xc_y_done.at(0, b))
            nc.vector.tensor_copy(xc_at[0:96, :, :], bank[0][0:96, 0:D].rearrange("p (s n) -> p s n", s=2))\
                .then_inc(xc_pt_ready.sem, 1)

        def dve_xc_out(dve, b):
            dve.wait_ge(xc_o_done.sem, xc_o_done.at(0, b + 1))
            for i in range(2):
                t = 2 * b + i
                dve.wait_ge(hb_ready.sem, hb_ready.at(LAYERS, t + 1 - NT))
                nc.vector.tensor_tensor(h[:, t, 0:D], bank[2][:, i * D:i * D + D], hb[:, t, :], ALU.add)\
                    .then_inc(xc_o_ready.sem, 1)

        def buffers(j):
            return (wb if j == 0 else wa), w2[j], b1[j], row_b2[j]

        def dve_first(ch, dst, src, n):
            bc = lambda m: m[:, :].unsqueeze(2).to_broadcast([P, NT, n])
            ch.link(nc.vector.tensor_reduce(gm[0][:, :], src, AX.X, ALU.max))
            ch.link(nc.vector.tensor_tensor(gt[1][:, :, 0:n], src, bc(gm[0]), ALU.is_equal))
            ch.link(nc.vector.tensor_tensor(gt[1][:, :, 0:n], gt[1][:, :, 0:n],
                                            prefer[:, 0:n].unsqueeze(1).to_broadcast([P, NT, n]), ALU.mult))
            ch.link(nc.vector.tensor_reduce(gm[1][:, :], gt[1][:, :, 0:n], AX.X, ALU.max))
            ch.link(nc.vector.tensor_tensor(dst, gt[1][:, :, 0:n], bc(gm[1]), ALU.is_equal))

        def sp_experts(sp, m, n, names):
            seg, w2n, b1n, b2n = names
            sg = moe[m]
            u_done, f_ready, y_done, y_read = sg["hidden"]
            with sp.Fori(0, n // 2) as it:
                for j in range(2):
                    e = 2 * it + j
                    _, w2j, b1j, b2j = buffers(j)
                    sp.wait_ge(sg["seg_ready"].sem, sg["seg_ready"].at(e, 0))
                    sp.dma_start(raw[:, :, :], a[seg][e, :, :, :]).then_inc(sg["seg_in"].sem, 16)
                    sp.wait_ge(y_done.sem, y_done.at(e, -NG * FC))
                    sp.wait_ge(y_read.sem, y_read.at(e, -NT))
                    sp.dma_start(w2j[:, :, :], a[w2n][e, :, :, :]).then_inc(sg["seg_in"].sem, 16)
                    sp.dma_start(b1j[:, :], a[b1n][e, :, :]).then_inc(sg["seg_in"].sem, 16)
                    sp.dma_start(b2j[:, :], a[b2n][e, :, :].to_broadcast([P, D])).then_inc(sg["seg_in"].sem, 16)

        def pool_experts(pool, ch, m, n, free):
            sg = moe[m]
            with pool.Fori(0, n // 2) as it:
                ch.enter(it, 64)
                for j in range(2):
                    e = 2 * it + j
                    free[j](pool)
                    pool.wait_ge(sg["hidden"][0].sem, sg["hidden"][0].at(e, -NG * FC))
                    pool.wait_ge(sg["seg_in"].sem, sg["seg_in"].at(e, 64))
                    alone(pool)
                    pool_weights(ch, buffers(j)[0], SEG).then_inc(sg["seg_ready"].sem, 1)
                ch.round_up()
            ch.leave(n // 2)

        def pe_experts(pe, m, n):
            with pe.Fori(0, n // 2) as it:
                for j in range(2):
                    e = 2 * it + j
                    w, w2j, _, _ = buffers(j)
                    pe.wait_ge(moe[m]["seg_ready"].sem, moe[m]["seg_ready"].at(e, 1))
                    pe_hidden(pe, e, None, w, w2j, moe[m]["hidden"], {})

        def act_experts(act, m, n, func):
            with act.Fori(0, n // 2) as it:
                for j in range(2):
                    act_hidden(act, 2 * it + j, None, buffers(j)[2], moe[m]["hidden"], func)

        def dve_experts(dve, ch, m, n):
            u_done, f_ready, y_done, y_read = moe[m]["hidden"]
            with dve.Fori(0, n // 2) as it:
                ch.enter(it, 512)
                for j in range(2):
                    e = 2 * it + j
                    dve.wait_ge(moe[m]["seg_ready"].sem, moe[m]["seg_ready"].at(e, 1))
                    for g in range(NG):
                        c = []
                        dve.wait_ge(y_done.sem, y_done.at(e, FC * (g + 1)))
                        for i in range(GT):
                            last = nc.vector.tensor_tensor(vf[:, i, :], bank[BY[i]][:, 0:D], row_b2[j][:, :], ALU.add)
                            last.then_inc(y_read.sem, 1)
                        for i in range(GT):
                            t = GT * g + i
                            dve.wait_ge(y_read.sem, y_read.at(e, t + 1))
                            c.append(ch.mark(nc.vector.scalar_tensor_tensor(
                                h[:, t, 0:D], in0=vf[:, i, :], scalar=gate[:, t, bass.ds(e, 1)], in1=h[:, t, 0:D],
                                op0=ALU.mult, op1=ALU.add)))
                        ch.done(c[-1])
                ch.round_up()
            ch.leave(n // 2)

        @block.sync
        def _(sp):
            for dst, src in ((ident, "ident"), (lo_rows, "lo_rows"), (lo_rows_q, "lo_rows_q"),
                             (lo_rows_q4, "neg_quarter"), (pad_keys, "pad_keys")):
                sp.dma_start(dst[:, :], a[src]).then_inc(const_in.sem, 16)
            for k, src in enumerate(("L0_tok_emb_ln_s", "L0_tok_emb_ln_b")):
                dst = (ln_s, ln_b)[k]
                sp.dma_start(dst[:, 1, :], a[src].unsqueeze(0).to_broadcast([P, D])).then_inc(const_in.sem, 16)
            sp.dma_start(hb[:, 0:2, :], a["L0_tok_emb_pos"]).then_inc(const_in.sem, 16)
            sp.dma_start(tok[:, :], a["x"]).then_inc(tok_in.sem, 16)
            sp.dma_start(xn[:, 0:8, :].bitcast(I32), a["mask_BS_i1_0"].unsqueeze(0).to_broadcast([P, B, S]))\
                .then_inc(mask_in.sem, 16)
            sp.dma_start(hb[:, 4:6, :], a["window"]).then_inc(mask_in.sem, 16)

            def load_x(it):
                sp.dma_start(raw[:, :, :], a["seg_a"][it, :, :, :]).then_inc(rows_x.sem, 16)
                sp.dma_start(row_bv[:, :], a["bv"][it, :, :].to_broadcast([P, D])).then_inc(rows_x.sem, 16)
                sp.dma_start(bqk[:, :], a["bqk"][it, :, :]).then_inc(rows_x.sem, 16)

            load_x(0)
            sp.dma_start(row_bo[:, :], a["bo"][0, :, :].to_broadcast([P, D])).then_inc(rows_bo.sem, 16)
            with sp.Fori(0, L) as it:
                sp.wait_ge(wa_ready.sem, wa_ready.at(it, 1))
                sp.wait_ge(h_ready.sem, h_ready.at(it, 0))
                sp.dma_start(raw[:, :, :], a["seg_b"][it, :, :, :]).then_inc(rows_y.sem, 16)
                sp.dma_start(w2[0][:, :, :], a["w2"][it, :, :, :]).then_inc(rows_y.sem, 16)
                sp.dma_start(b1[0][:, :], a["b1"][it, :, :]).then_inc(rows_y.sem, 16)
                for dst, src in ((row_b2[0][:, :], "b2"), (ln_s[:, 0, :], "ln1_s"), (ln_b[:, 0, :], "ln1_b"),
                                 (ln_s[:, 1, :], "ln2_s"), (ln_b[:, 1, :], "ln2_b")):
                    sp.dma_start(dst, a[src][it, :, :].to_broadcast([P, D])).then_inc(rows_y.sem, 16)
                sp.wait_ge(hb_ready.sem, hb_ready.at(it, 0))
                sp.dma_start(row_bo[:, :], a["bo"][it + 1, :, :].to_broadcast([P, D])).then_inc(rows_bo.sem, 16)
                sp.wait_ge(wb_ready.sem, wb_ready.at(it, 1))
                sp.wait_ge(proj_done.sem, proj_done.at(it, 10 * NG))
                sp.wait_ge(vf_ready.sem, vf_ready.at(it, 4 * NG))
                sp.wait_ge(qf_ready.sem, qf_ready.at(it, 6 * NG))
                load_x(it + 1)
            sp.wait_ge(wa_ready.sem, wa_ready.at(L, 1))
            sp.wait_ge(h_ready.sem, h_ready.at(L, 0))
            for dst, src in ((xc_temp[:, :], "xc_temp"), (xc_mask[:, :, :], "xc_mask"), (xc_wp[:, :, :], "xc_wp"),
                             (prefer[:, :], "prefer"), (br1[:, :], "br1"), (wr2[:, :, :], "wr2"),
                             (row_bg[:, :], "bg"), (row_br2[:, :], "br2")):
                if src in ("bg", "br2"):
                    src = a[src].unsqueeze(0).to_broadcast([P, dst.shape[1]])
                else:
                    src = a[src]
                sp.dma_start(dst, src).then_inc(aux_in.sem, 16)
            sp_experts(sp, 0, 4, ("e0_seg", "e0_w2", "e0_b1", "e0_b2"))
            sp.wait_ge(moe[0]["seg_ready"].sem, moe[0]["seg_ready"].at(0, 4))
            sp.dma_start(raw[:, :, :], a["seg_q"]).then_inc(seg_q_in.sem, 16)
            sp.wait_ge(seg_q_ready.sem, seg_q_ready.at(0, 1))
            sp.dma_start(raw[:, :, 0:D], a["seg_p"]).then_inc(seg_q_in.sem, 16)
            sp.wait_ge(hb_ready.sem, hb_ready.at(L, 0))
            sp.dma_start(row_bo[:, :], a["bproj"].unsqueeze(0).to_broadcast([P, D])).then_inc(rows_bo.sem, 16)
            sp.wait_ge(seg_q_ready.sem, seg_q_ready.at(0, 2))
            sp.wait_ge(sum_ready.sem, sum_ready.at(0, 1))
            sp_experts(sp, 1, 8, ("e1_seg", "e1_w2", "e1_b1", "e1_b2"))
            sp.wait_ge(sum_ready.sem, sum_ready.at(0, 2))
            if stop is None:
                sp.dma_start(out.rearrange("(t p) d -> p t d", p=P), h[:, :, 0:D]).then_inc(out_done.sem, 16)
                sp.wait_ge(out_done.sem, 16)
            if stop == "tok":
                sp.wait_ge(h_ready.sem, h_ready.at(L, 0))
                sp.dma_start(out.rearrange("(t p) d -> p t d", p=P), h[:, :, 0:D]).then_inc(out_done.sem, 16)
                sp.wait_ge(out_done.sem, 16)

        @block.gpsimd
        def _(pool):
            ch = Chain(ctx, nc, pool, "pool_order", alone)
            for s in (v3_ready, moe[0]["seg_ready"], moe[1]["seg_ready"], xc_pow_ready, seg_q_ready):
                s.start(pool)
            nc.gpsimd.memset(neg_half[:, :], -0.5)
            nc.gpsimd.memset(prob[:, 0, :, D:2 * P], 0.0)
            nc.gpsimd.memset(prob[:, 1, :, 0:WIN], 0.0).then_inc(zeroed.sem, 1)
            pool.wait_ge(zeroed.sem, 1)
            pool.wait_ge(tok_ok.sem, 1)
            for t in range(NT):
                pool.indirect_dma_start(out=h[:, t, 0:D], out_offset=None, in_=a["L0_tok_emb_word"],
                                        in_offset=bass.IndirectOffsetOnAxis(ap=toku[:, t:t + 1], axis=0))\
                    .then_inc(gathered.sem, 16)
            pool.wait_ge(rows_x.sem, 48)
            pool_weights(ch, wa, SEG).then_inc(wa_ready.sem, 1)
            pool.wait_ge(rows_bo.sem, 16)
            for g in range(NG + 1):
                if g < NG:
                    pool_rstd(pool, ch, 0, g + 1 - NG, g, 1e-12)
                if g:
                    if g == 1:
                        pool.wait_ge(mask_ok.sem, 1)
                    pool_hb(pool, 0, -NT, g - 1, row_bo)
            with pool.Fori(0, L) as it:
                ch.enter(it, 128)
                pool_v(pool, ch, it, 0)
                pool_v(pool, ch, it, 1)
                pool.wait_ge(rows_y.sem, rows_y.at(it, 16 * 8))
                alone(pool)
                pool_weights(ch, wb, SEG).then_inc(wb_ready.sem, 1)
                pool_v(pool, ch, it, 2)
                pool_v(pool, ch, it, 3)
                pool.wait_ge(rows_x.sem, rows_x.at(it + 1, 48))
                alone(pool)
                pool_weights(ch, wa, SEG).then_inc(wa_ready.sem, 1)
                for g in range(NG + 1):
                    if g < NG:
                        pool_rstd(pool, ch, it, g + 1, g, 1e-12)
                    if g:
                        pool_hb(pool, it, 0, g - 1, row_b2[0])
                pool.wait_ge(rows_bo.sem, rows_bo.at(it + 1, 16))
                for g in range(NG + 1):
                    if g < NG:
                        pool_rstd(pool, ch, it, NG + g + 1, g, 1e-12)
                    if g:
                        pool_hb(pool, it, NT, g - 1, row_bo)
                ch.round_up()
            ch.leave(L)
            nc.gpsimd.memset(xc_nh[:, :], -0.5)
            nc.gpsimd.memset(xc_one[:, :], 1.0).then_inc(zeroed.sem, 1)
            pool.wait_ge(zeroed.sem, 2)
            for g in range(NG):
                pool_rstd(pool, ch, L, g + 1, g, 1e-5)
            for b in range(B):
                pool.wait_ge(xc_norm_ready.sem, xc_norm_ready.at(0, b + 1))
                pool.wait_ge(xc_s_ready.sem, xc_s_ready.at(0, b))
                nc.gpsimd.tensor_tensor(xc_norm[0:96, 1, :], xc_norm[0:96, 0, :], xc_nh[0:96, :], ALU.pow)\
                    .then_inc(xc_pow_ready.sem, 1)
            for g in range(NG):
                pool_rstd(pool, ch, L, NG + g + 1, g, 1e-5)
            pool_experts(pool, ch, 0, 4,
                         (lambda e: e.wait_ge(u_done.sem, u_done.at(L - 1, NG * FC)), lambda e: e.wait_ge(gates_done.sem, gates_done.at(0, 1))))
            pool.wait_ge(seg_q_in.sem, seg_q_in.at(0, 16))
            pool.wait_ge(moe[0]["hidden"][0].sem, moe[0]["hidden"][0].at(2, NG * FC))
            pool_weights(ch, wb, SEG).then_inc(seg_q_ready.sem, 1)
            pool.wait_ge(seg_q_in.sem, seg_q_in.at(0, 32))
            pool.wait_ge(moe[0]["hidden"][0].sem, moe[0]["hidden"][0].at(3, NG * FC))
            pool_weights(ch, wa, D).then_inc(seg_q_ready.sem, 1)
            pool.wait_ge(rows_bo.sem, rows_bo.at(L + 1, 16))
            pool.wait_ge(sum_ready.sem, sum_ready.at(0, 1))
            for t in range(NT):
                nc.gpsimd.tensor_tensor(hb[:, t, :], h[:, t, 0:D], row_bo[:, :], ALU.add).then_inc(hb_ready.sem, 1)
            for g in range(NG):
                pool_rstd(pool, ch, L + 1, g + 1, g, 1e-5)
            for g in range(NG):
                pool_v(pool, ch, L, g)
            for g in range(NG):
                pool_rstd(pool, ch, L + 1, NG + g + 1, g, 1e-5)
            pool_experts(pool, ch, 1, 8,
                         (lambda e: e.wait_ge(proj_done.sem, proj_done.at(L, 10 * NG)), lambda e: e.wait_ge(o_done.sem, o_done.at(L, NT))))

        @block.scalar
        def _(act):
            for s in (xh_ready, qf_ready, exp_done, pad_ready, hi_ready, f_ready, moe[0]["hidden"][1],
                      moe[1]["hidden"][1], xc_qk_ready, xc_v_ready, xc_e_ready, xc_y_ready, r_ready, g2_exp):
                s.start(act)
            act.wait_ge(const_in.sem, 16 * 8)
            with act.Fori(0, L) as it:
                for t in range(GT):
                    act_split(act, it, 0, t)
                act_attention(act, it, True, beside(lambda t: act_split(act, it, 0, t)))
                for t in range(NT):
                    act_split(act, it, 1, t)
                act_hidden(act, it, 2, b1[0], tok_hidden, ACT.Gelu)
            for t in range(NT):
                act_split(act, L, 0, t)
            for b in range(B + 1):
                if b < B:
                    act_xc_front(act, b)
                if b:
                    act_xc_exp(act, b - 1)
                    act_xc_back(act, b - 1)
            for t in range(NT):
                act_split(act, L, 1, t)
            act_experts(act, 0, 4, ACT.Gelu)
            for t in range(GT):
                act_split(act, L, 2, t)
            act_attention(act, L, False, beside(lambda t: act_split(act, L, 2, t)))
            for t in range(NT):
                act_split(act, L + 1, 0, t)
            for t in range(NT):
                act_split(act, L + 1, 1, t)
            for g in range(NG):
                for s in range(2):
                    act.wait_ge(r_done.sem, r_done.at(0, 2 * g + s + 1))
                    act.wait_ge(g2_done.sem, g2_done.at(0, GT * (g - 1)))
                    m = P if s == 0 else D2
                    nc.scalar.activation(fbuf[0:m, 2 * (g % 2) + s, :], bank[BU[s]][0:m, :], ACT.Relu,
                                         bias=br1[0:m, s:s + 1]).then_inc(r_ready.sem, 1)
            act.wait_ge(g2_max.sem, g2_max.at(0, 1))
            nc.scalar.activation(gt[2][:, :, :], gt[2][:, :, :], ACT.Exp).then_inc(g2_exp.sem, 1)
            act_experts(act, 1, 8, ACT.Relu)

        @block.vector
        def _(dve):
            ch = Chain(ctx, nc, dve, "dve_order")
            for s in (xx_ready, qk_ready, vf_ready, max_ready, lo_ready, att_ready, o_read, y_read,
                      moe[0]["hidden"][3], moe[1]["hidden"][3], xn_ready, xc_norm_ready, xc_k_ready, xc_s_ready, xc_p_ready,
                      xc_pt_ready, xc_o_ready, gates_ready, g2_max, sum_ready):
                s.start(dve)
            dve.wait_ge(tok_in.sem, 16)
            ch.link(nc.vector.tensor_copy(tokf[:, 0, :], tok[:, :]))
            ch.link(nc.vector.tensor_scalar(tokf[:, 1, :], tokf[:, 0, :], 0.0, float(VOCAB), ALU.is_lt, ALU.mult))
            ch.link(nc.vector.tensor_tensor(tokf[:, 0, :], tokf[:, 0, :], tokf[:, 1, :], ALU.add))
            ch.link(nc.vector.tensor_scalar(tokf[:, 1, :], tokf[:, 0, :], 0.0, float(VOCAB - 1), ALU.max, ALU.min))
            nc.vector.tensor_copy(toku[:, :], tokf[:, 1, :]).then_inc(tok_ok.sem, 1)
            dve.wait_ge(mask_in.sem, 32)
            km = xn[:, 8:16, :]
            ch.link(nc.vector.tensor_copy(km, xn[:, 0:8, :].bitcast(I32)))
            ch.link(nc.vector.tensor_scalar(xn[:, 0:8, :], km, 0.0, -1.0, ALU.is_gt, ALU.add))
            ch.link(nc.vector.tensor_scalar(km, xn[:, 0:8, :], -NEG_IN, None, ALU.mult))
            for t in range(NT):
                qt = t % 2
                last = nc.vector.tensor_tensor(mask[:, t, :], hb[:, 4 + qt, :],
                                               km[:, t // 2, qt * WIN:qt * WIN + D], ALU.min)
                ch.mark(last)
            ch.done(ch.n)
            dve.wait_ge(const_in.sem, 16 * 8)
            dve.wait_ge(gathered.sem, 16 * NT)
            for t in range(NT):
                ch.mark(nc.vector.tensor_tensor(h[:, t, 0:D], h[:, t, 0:D], hb[:, t % 2, :], ALU.add))
            ch.done(ch.n)
            dve.sem_inc(mask_ok.sem, 1)
            for g in range(NG + 1):
                if g < NG:
                    dve_stats(dve, ch, 0, 0, g, None)
                if g:
                    dve_affine(dve, ch, 0, 0, g - 1, 1)
            with dve.Fori(0, L) as it:
                ch.enter(it, 512)
                for t in range(GT):
                    dve_split(dve, it, 0, t)
                dve_attention(dve, ch, it, True, beside(lambda t: dve_split(dve, it, 0, t)))
                dve.wait_ge(rows_y.sem, rows_y.at(it, 16 * 8))
                for g in range(NG + 2):
                    if g < NG:
                        for t in range(GT * g, GT * g + GT):
                            dve_split(dve, it, 1, t)
                    if 1 <= g <= NG:
                        dve_residual(dve, ch, it, 0, g - 1)
                        dve_stats(dve, ch, it, 0, g - 1, o_read)
                    if g >= 2:
                        dve_affine(dve, ch, it, 1, g - 2, 0)
                for t in range(NT):
                    dve_split(dve, it, 2, t)
                for g in range(NG + 1):
                    if g < NG:
                        dve_residual(dve, ch, it, 1, g)
                        dve_stats(dve, ch, it, 1, g, y_read)
                    if g:
                        dve_affine(dve, ch, it, 2, g - 1, 1)
                ch.round_up()
            ch.leave(L)
            dve.wait_ge(aux_in.sem, 16 * 8)
            dve_norm_in(dve, ch, L, 0, 0)
            for b in range(B + 1):
                if b:
                    dve_xc_probs(dve, ch, b - 1)
                if b < B:
                    dve_xc_logits(dve, ch, b)
                if b:
                    dve_xc_out(dve, b - 1)
            dve.wait_ge(xc_o_ready.sem, xc_o_ready.at(0, NT))
            dve_norm_in(dve, ch, L, 1, 1)
            dve.wait_ge(gates_done.sem, gates_done.at(0, 1))
            ch.link(nc.vector.tensor_tensor(gt[0][:, :, 0:4], bank[2][:, 0:4 * NT].rearrange("p (t n) -> p t n", n=4),
                                            row_bg[:, :].unsqueeze(1).to_broadcast([P, NT, 4]), ALU.add))
            dve_first(ch, gate[:, :, 0:4], gt[0][:, :, 0:4], 4)
            dve.sem_inc(gates_ready.sem, 1)
            dve_experts(dve, ch, 0, 4)
            dve.sem_inc(sum_ready.sem, 1)
            dve_norm_in(dve, ch, L + 1, 0, None)
            for t in range(GT):
                dve_split(dve, L, 2, t)
            dve_attention(dve, ch, L, False, beside(lambda t: dve_split(dve, L, 2, t)))
            for g in range(NG + 1):
                if g < NG:
                    for t in range(GT * g, GT * g + GT):
                        dve_split(dve, L + 1, 0, t)
                if g:
                    dve_residual(dve, ch, L, 0, g - 1, 1)
            dve.wait_ge(o_read.sem, o_read.at(L, NT))
            dve_norm_in(dve, ch, L + 1, 1, 1)
            dve.wait_ge(g2_done.sem, g2_done.at(0, NT))
            ch.link(nc.vector.tensor_tensor(gt[0][:, :, :], bank[4][:, 0:8 * NT].rearrange("p (t n) -> p t n", n=8),
                                            row_br2[:, :].unsqueeze(1).to_broadcast([P, NT, 8]), ALU.add))
            dve_first(ch, gate[:, :, :], gt[0][:, :, :], 8)
            nc.vector.tensor_tensor(gt[2][:, :, :], gt[0][:, :, :],
                                    gm[0][:, :].unsqueeze(2).to_broadcast([P, NT, 8]), ALU.subtract)\
                .then_inc(g2_max.sem, 1)
            ch.link(nc.vector.scalar_tensor_tensor(gt[0][:, :, :], in0=gate[:, :, :], scalar=NEG_OUT,
                                                   in1=gt[0][:, :, :], op0=ALU.mult, op1=ALU.add))
            dve_first(ch, gt[1][:, :, :], gt[0][:, :, :], 8)
            ch.link(nc.vector.tensor_tensor(gate[:, :, :], gate[:, :, :], gt[1][:, :, :], ALU.add))
            dve.wait_ge(g2_exp.sem, g2_exp.at(0, 1))
            ch.link(nc.vector.tensor_tensor(gt[0][:, :, :], gate[:, :, :], gt[2][:, :, :], ALU.mult))
            ch.link(nc.vector.tensor_reduce(gm[0][:, :], gt[0][:, :, :], AX.X, ALU.add))
            ch.link(nc.vector.reciprocal(gm[1][:, :], gm[0][:, :]))
            ch.link(nc.vector.tensor_tensor(gate[:, :, :], gt[0][:, :, :],
                                            gm[1][:, :].unsqueeze(2).to_broadcast([P, NT, 8]), ALU.mult))
            dve_experts(dve, ch, 1, 8)
            dve.sem_inc(sum_ready.sem, 1)

        @block.tensor
        def _(pe):
            for s in (xt_done, proj_done, s_done, t_done, pv_done, o_done, u_done, y_done, moe[0]["hidden"][0],
                      moe[0]["hidden"][2], moe[1]["hidden"][0], moe[1]["hidden"][2], xc_qk_done, xc_v_done,
                      xc_gram_done, xc_kt_done, xc_pt_done, xc_y_done, xc_o_done, gates_done, r_done, g2_done):
                s.start(pe)
            pe.wait_ge(const_in.sem, 16 * 8)
            pe.wait_ge(zeroed.sem, 1)
            with pe.Fori(0, L) as it:
                for t in range(GT):
                    pe_transpose(pe, it, 0, t, h, h_ready, it, t + 1 - NT)
                pe.wait_ge(wa_ready.sem, wa_ready.at(it, 1))
                pe.wait_ge(xx_ready.sem, xx_ready.at(it, GT))
                pe_attention(pe, it, True, wa, beside(
                    lambda t: pe_transpose(pe, it, 0, t, h, h_ready, it, t + 1 - NT), lambda n: (it, n)))
                pe.wait_ge(wb_ready.sem, wb_ready.at(it, 1))
                for g in range(NG + 1):
                    if g < NG:
                        for t in range(GT * g, GT * g + GT):
                            pe_transpose(pe, it, 1, t, xn, att_ready, it, t + 1)
                    if g:
                        pe_out(pe, it, wb, 0, g - 1, lambda t: (it, NT + t + 1))
                for t in range(2 * GT):
                    pe_transpose(pe, it, 2, t, h, h_ready, it, t + 1)

                def later(g):
                    for t in range(GT * g, GT * g + GT):
                        pe_transpose(pe, it, 2, t, h, h_ready, it, t + 1)

                pe_hidden(pe, it, 2, wb, w2[0], tok_hidden, {2: lambda: later(2), 4: lambda: later(3)})


            for t in range(NT):
                pe_transpose(pe, L, 0, t, xn, xn_ready, 0, t + 1)
            pe.wait_ge(wa_ready.sem, wa_ready.at(L, 1))
            pe.wait_ge(xx_ready.sem, xx_ready.at(L, NT))
            pe.wait_ge(aux_in.sem, 16 * 8)
            pe.wait_ge(zeroed.sem, 2)
            for b in range(B + 1):
                if b < B:
                    pe_xc_front(pe, b)
                    pe_xc_gram(pe, b)
                if b:
                    pe_xc_back(pe, b - 1)
                if b < B:
                    pe_xc_turn(pe, b)
            for t in range(NT):
                pe_transpose(pe, L, 1, t, xn, xn_ready, 0, NT + t + 1)
            pe.wait_ge(xx_ready.sem, xx_ready.at(L, 2 * NT))
            for t in range(NT):
                last = pe_tokens(bank[2][:, 4 * t:4 * t + 4], wa, 3 * D, 4, t)
            last.then_inc(gates_done.sem, 1)
            pe.wait_ge(gates_ready.sem, gates_ready.at(0, 1))
            pe_experts(pe, 0, 4)
            for t in range(GT):
                pe_transpose(pe, L, 2, t, xn, xn_ready, 0, 2 * NT + t + 1)
            pe.wait_ge(seg_q_ready.sem, seg_q_ready.at(0, 1))
            pe.wait_ge(xx_ready.sem, xx_ready.at(L, 2 * NT + GT))
            pe_attention(pe, L, False, wb, beside(
                lambda t: pe_transpose(pe, L, 2, t, xn, xn_ready, 0, 2 * NT + t + 1), lambda n: (L, 2 * NT + n)))
            pe.wait_ge(seg_q_ready.sem, seg_q_ready.at(0, 2))
            for g in range(NG + 1):
                if g < NG:
                    for t in range(GT * g, GT * g + GT):
                        pe_transpose(pe, L + 1, 0, t, xn, att_ready, L, t + 1)
                if g:
                    pe_out(pe, L, wa, 0, g - 1, lambda t: (L + 1, t + 1))
            for t in range(NT):
                pe_transpose(pe, L + 1, 1, t, xn, xn_ready, 0, 3 * NT + t + 1)
            pe.wait_ge(moe[1]["seg_ready"].sem, moe[1]["seg_ready"].at(0, 1))
            pe.wait_ge(xx_ready.sem, xx_ready.at(L + 1, 2 * NT))
            for g in range(NG + 1):
                if g < NG:
                    for s in range(2):
                        pe.wait_ge(r_ready.sem, r_ready.at(0, 2 * (g - 1) + s + 1))
                        pe_features(bank[BU[s]][:, :], wb, s * P, g).then_inc(r_done.sem, 1)
                if g:
                    pe.wait_ge(r_ready.sem, r_ready.at(0, 2 * g))
                    for t in range(GT * (g - 1), GT * g):
                        tk = slice(t % GT * P, t % GT * P + P)
                        f = 2 * ((g - 1) % 2)
                        o = bank[4][:, 8 * t:8 * t + 8]
                        nc.tensor.matmul(o, fbuf[:, f, tk], wr2[:, 0, :], start=True, stop=False)
                        nc.tensor.matmul(o, fbuf[0:D2, f + 1, tk], wr2[0:D2, 1, :], start=False, stop=True)\
                            .then_inc(g2_done.sem, 1)
            pe.wait_ge(g2_max.sem, g2_max.at(0, 1))
            pe_experts(pe, 1, 8)


def pack_segment(*parts):
    w = np.concatenate(parts, axis=-1)
    w = np.concatenate([w, np.zeros(w.shape[:-1] + (SEG - w.shape[-1],), w.dtype)], axis=-1)
    return np.stack([w[..., :P, :], np.concatenate([w[..., P:, :], w[..., P:, :]], axis=-2)], axis=-2)


def pack_heads(w):
    w = w.reshape(w.shape[:-1] + (HEADS, 1, DH))
    return np.concatenate([w, w], axis=-2).reshape(w.shape[:-3] + (HEADS * 2 * DH,))


def lay_out(i):
    n = {k: np.asarray(v) for k, v in i.items()}
    g = lambda k: n["L0_tok_" + k]
    o = {}
    row = np.arange(P)
    o["ident"] = np.eye(P, dtype=np.float32)
    o["lo_rows"] = -(row >= 64).astype(np.float32)[:, None]
    o["lo_rows_q"] = -(row % 32 >= 16).astype(np.float32)[:, None]
    o["neg_quarter"] = np.full((P, 1), np.float32(NEG_IN) / 4, np.float32)
    o["pad_keys"] = np.stack([(row < WIN) * WIN, (row >= WIN) * WIN], 1).astype(np.float32)
    k = np.arange(D)[None, :]
    win = []
    for qt in range(2):
        q, key = qt * P + row[:, None], qt * WIN + k
        m = np.where(np.abs(q - key) <= WIN, 3e38, NEG_IN)
        out_of = (key < (q // WIN - 1) * WIN) | (key >= (q // WIN + 2) * WIN)
        win.append(np.where(out_of, NEG_OUT, m))
    o["window"] = np.stack(win, 1).astype(np.float32)
    o["x"] = np.ascontiguousarray(n["x"].reshape(NT, P).T)
    o["mask_BS_i1_0"] = n["mask_BS_i1_0"]
    o["L0_tok_emb_word"] = g("emb_word")
    o["L0_tok_emb_pos"] = np.ascontiguousarray(g("emb_pos")[:S].reshape(2, P, D).transpose(1, 0, 2))
    o["L0_tok_emb_ln_s"], o["L0_tok_emb_ln_b"] = g("emb_ln_s"), g("emb_ln_b")
    xc = n["L0_attn_W_qkv"].reshape(D, D, 3).transpose(0, 2, 1).reshape(D, 3 * D)
    xc = np.concatenate([xc, n["L0_ffn_Wg"]], axis=-1)
    seg_a = pack_segment(pack_heads(g("Wq")), pack_heads(g("Wk")), g("Wv"))
    o["seg_a"] = np.concatenate([seg_a, pack_segment(xc)[None]])
    o["seg_b"] = pack_segment(g("Wo"), g("W1"))
    o["w2"] = g("W2").reshape(LAYERS, FC, P, D).transpose(0, 2, 1, 3)
    bqk = np.concatenate([pack_heads(g("bq")), pack_heads(g("bk"))], -1).reshape(LAYERS, 6, P)
    o["bqk"] = np.concatenate([bqk, np.zeros_like(bqk[:1])]).transpose(0, 2, 1)
    o["b1"] = g("b1").reshape(LAYERS, FC, P).transpose(0, 2, 1)
    o["bv"] = np.concatenate([g("bv"), np.zeros_like(g("bv")[:1])])[:, None]
    o["bo"] = np.concatenate([g("bo"), n["L0_attn_b_proj"][None]])[:, None]
    for k in ("b2", "ln1_s", "ln1_b", "ln2_s", "ln2_b"):
        o[k] = g(k)[:, None]
    pad = lambda w: np.concatenate([w, np.zeros((P - 96,) + w.shape[1:], w.dtype)])
    temp = np.repeat(n["L0_attn_temp"].reshape(XC_H), XC_D).reshape(2, 96)
    o["xc_temp"] = pad(temp.T)
    c = np.arange(96) // XC_D
    block = np.where(c[:, None] == c[None, :], 0.0, NEG_IN).astype(np.float32)
    o["xc_mask"] = pad(np.stack([block, block], 1))
    o["xc_wp"] = pad(n["L0_attn_W_proj"].reshape(2, 96, D).transpose(1, 0, 2))
    o["prefer"] = np.tile(np.arange(8, 0, -1, dtype=np.float32), (P, 1))
    two = lambda w: np.stack([w[:P], np.concatenate([w[P:], np.zeros((P - D2,) + w.shape[1:], w.dtype)])], 1)
    o["br1"] = two(n["L1_ffn_br1"])
    o["wr2"] = two(n["L1_ffn_Wr2"].T)
    o["bg"], o["br2"] = n["L0_ffn_bg"], n["L1_ffn_br2"]
    zero = np.zeros((D, D), np.float32)
    o["e0_seg"] = np.stack([pack_segment(zero, w) for w in n["L0_ffn_W1"]])
    o["e0_w2"] = n["L0_ffn_W2"].reshape(4, FC, P, D).transpose(0, 2, 1, 3)
    o["e0_b1"] = n["L0_ffn_b1"].reshape(4, FC, P).transpose(0, 2, 1)
    o["e0_b2"] = n["L0_ffn_b2"][:, None]
    w1 = n["L1_ffn_W1"].transpose(0, 2, 1)
    o["e1_seg"] = np.stack([pack_segment(n["L1_ffn_Wr1"].T if e == 0 else zero, w) for e, w in enumerate(w1)])
    o["e1_w2"] = n["L1_ffn_W2"].transpose(0, 2, 1).reshape(8, FC, P, D).transpose(0, 2, 1, 3)
    o["e1_b1"] = n["L1_ffn_b1"].reshape(8, FC, P).transpose(0, 2, 1)
    o["e1_b2"] = n["L1_ffn_b2"][:, None]
    wq, wk, wv = np.split(n["L1_attn_Wqkv"], 3, axis=1)
    o["seg_q"] = pack_segment(pack_heads(wq), pack_heads(wk), wv)
    o["seg_p"] = pack_segment(n["L1_attn_Wproj"])[:, :, :D]
    o["bproj"] = n["L1_attn_bproj"]
    return {k: np.ascontiguousarray(v) for k, v in o.items()}


def kernel(**inputs):
    import concourse.bacc as bacc
    from concourse.bass_utils import run_bass_kernel_spmd

    nc = bacc.Bacc("TRN2", target_bir_lowering=False, num_devices=1)
    arrays, args = {}, {}
    for name, v in lay_out(inputs).items():
        arrays[f"in_{name}"] = v
        args[name] = nc.dram_tensor(f"in_{name}", v.shape, mybir.dt.from_np(v.dtype), kind="ExternalInput").ap()
    out = nc.dram_tensor("out_0", (NT * P, D), F32, kind="ExternalOutput").ap()
    build_tower(nc, args, out)
    r = run_bass_kernel_spmd(nc, [arrays], core_ids=[0])
    return r.results[0]["out_0"].reshape(B, S, D)
```
